# Optimizing a Trainium2 kernel written in Bass

```python
import numpy as np
import jax
import jax.numpy as jnp

def _softmax(x, axis=-1):
    return jax.nn.softmax(x, axis=axis)

def _gelu(x):
    return jax.nn.gelu(x, approximate=True)

def _silu(x):
    return jax.nn.silu(x)

def _sigmoid(x):
    return jax.nn.sigmoid(x)

def _layernorm(x, axis=-1, eps=1e-05):
    m = jnp.mean(x, axis=axis, keepdims=True)
    v = jnp.var(x, axis=axis, keepdims=True)
    return (x - m) / jnp.sqrt(v + eps)

def _scatter_add(tgt, idx, src, axis=0):
    return tgt.at[idx].add(src)

def _segment_sum(src, seg, n):
    return jax.ops.segment_sum(src, seg, n)
kernel_name = 'mk_recurrent_d1_jaxref_r8_7c90e2'

def setup_inputs(seed: int=0):
    np.random.seed(seed)
    _w = jnp.asarray

    def _L0_attn_setup():
        import jax, jax.numpy as jnp
        import numpy as np
        D_MODEL = 256
        NUM_HEADS = 16
        HEAD_DIM = D_MODEL // NUM_HEADS
        SCALE = HEAD_DIM ** (-0.5)
        ALPHA = 1.0
        key = jax.random.key(seed)
        ks = jax.random.split(key, 9)
        B, T = (2, 256)
        s = 0.02
        w = lambda k: jax.random.normal(k, (D_MODEL, D_MODEL), jnp.float32) * s
        b = lambda k: jax.random.normal(k, (D_MODEL,), jnp.float32) * s
        return {'x': jax.random.normal(ks[0], (B, T, D_MODEL), jnp.float32), 'q_w': w(ks[1]), 'q_b': b(ks[2]), 'k_w': w(ks[3]), 'k_b': b(ks[4]), 'v_w': w(ks[5]), 'v_b': b(ks[6]), 'o_w': w(ks[7]), 'o_b': b(ks[8])}
    _L0_attn_in = _L0_attn_setup()

    def _L0_ffn_setup():
        import jax, jax.numpy as jnp
        import numpy as np
        NUM_EXPERTS = 8
        HIDDEN = 256
        INTER = 256
        TOP_K = 2
        key = jax.random.key(seed)
        ks = jax.random.split(key, 7)
        hidden_states = jax.random.normal(ks[0], (4, 256, HIDDEN), dtype=jnp.float32)
        gate_w = jax.random.normal(ks[1], (HIDDEN, NUM_EXPERTS), dtype=jnp.float32) * 0.02
        fc1_w = jax.random.normal(ks[2], (NUM_EXPERTS, HIDDEN, INTER), dtype=jnp.float32) * 0.02
        fc1_b = jnp.zeros((NUM_EXPERTS, INTER), dtype=jnp.float32)
        fc2_w = jax.random.normal(ks[3], (NUM_EXPERTS, INTER, HIDDEN), dtype=jnp.float32) * 0.02
        fc2_b = jnp.zeros((NUM_EXPERTS, HIDDEN), dtype=jnp.float32)
        alpha = jax.random.normal(ks[4], (NUM_EXPERTS,), dtype=jnp.float32)
        return {'hidden_states': hidden_states, 'gate_w': gate_w, 'fc1_w': fc1_w, 'fc1_b': fc1_b, 'fc2_w': fc2_w, 'fc2_b': fc2_b, 'alpha': alpha}
    _L0_ffn_in = _L0_ffn_setup()
    _d = {'L0_attn_x': _L0_attn_in['x'], 'L0_attn_q_w': _L0_attn_in['q_w'], 'L0_attn_q_b': _L0_attn_in['q_b'], 'L0_attn_k_w': _L0_attn_in['k_w'], 'L0_attn_k_b': _L0_attn_in['k_b'], 'L0_attn_v_w': _L0_attn_in['v_w'], 'L0_attn_v_b': _L0_attn_in['v_b'], 'L0_attn_o_w': _L0_attn_in['o_w'], 'L0_attn_o_b': _L0_attn_in['o_b'], 'L0_ffn_gate_w': _L0_ffn_in['gate_w'], 'L0_ffn_fc1_w': _L0_ffn_in['fc1_w'], 'L0_ffn_fc1_b': _L0_ffn_in['fc1_b'], 'L0_ffn_fc2_w': _L0_ffn_in['fc2_w'], 'L0_ffn_fc2_b': _L0_ffn_in['fc2_b'], 'L0_ffn_alpha': _L0_ffn_in['alpha']}
    _x0 = _d['L0_attn_x']
    _d['L0_attn_x'] = jax.random.normal(jax.random.fold_in(jax.random.key(seed), 1), (4, 1024, 256), dtype=_x0.dtype)
    del _x0
    return _d

def reference(L0_attn_x, L0_attn_q_w, L0_attn_q_b, L0_attn_k_w, L0_attn_k_b, L0_attn_v_w, L0_attn_v_b, L0_attn_o_w, L0_attn_o_b, L0_ffn_gate_w, L0_ffn_fc1_w, L0_ffn_fc1_b, L0_ffn_fc2_w, L0_ffn_fc2_b, L0_ffn_alpha):

    def _L0_attn_ref(x, q_w, q_b, k_w, k_b, v_w, v_b, o_w, o_b):
        import jax, jax.numpy as jnp
        import numpy as np
        D_MODEL = 256
        NUM_HEADS = 16
        HEAD_DIM = D_MODEL // NUM_HEADS
        SCALE = HEAD_DIM ** (-0.5)
        ALPHA = 1.0
        B, T, D = x.shape
        H, HD = (NUM_HEADS, HEAD_DIM)

        def proj_split(w, bias):
            y = x @ w.T + bias
            return y.reshape(B, T, H, HD).transpose(0, 2, 1, 3).reshape(B * H, T, HD)
        Q = proj_split(q_w, q_b)
        K = proj_split(k_w, k_b)
        V = proj_split(v_w, v_b)
        S = jnp.einsum('hid,hjd->hij', K, Q) * SCALE
        idx = jnp.arange(T)
        delta = idx[:, None] - idx[None, :]
        decay = jnp.where(delta < 0, 0.0, -delta.astype(jnp.float32) ** ALPHA)
        S = jnp.where(delta < 0, -jnp.inf, S) + decay
        C = jax.nn.softmax(S, axis=-1)
        attn = jnp.einsum('hij,hjd->hid', C, V)
        attn = attn.reshape(B, H, T, HD).transpose(0, 2, 1, 3).reshape(B, T, D)
        return attn @ o_w.T + o_b

    def _L0_ffn_ref(hidden_states, gate_w, fc1_w, fc1_b, fc2_w, fc2_b, alpha):
        import jax, jax.numpy as jnp
        import numpy as np
        NUM_EXPERTS = 8
        HIDDEN = 256
        INTER = 256
        TOP_K = 2
        B, S, H = hidden_states.shape
        x = hidden_states.reshape(-1, H)
        probs = jax.nn.softmax(x @ gate_w, axis=-1)
        gate_score, gate_idx = jax.lax.top_k(probs, TOP_K)
        gate_score = gate_score / jnp.sum(gate_score, axis=-1, keepdims=True)
        onehot = jax.nn.one_hot(gate_idx, NUM_EXPERTS, dtype=x.dtype)
        combine = jnp.einsum('tk,tke->te', gate_score, onehot) * alpha[None, :]
        h = jnp.einsum('th,ehi->eti', x, fc1_w) + fc1_b[:, None, :]
        h = jax.nn.gelu(h, approximate=False)
        y = jnp.einsum('eti,eih->eth', h, fc2_w) + fc2_b[:, None, :]
        out = jnp.einsum('eth,te->th', y, combine)
        return out.reshape(B, S, H)
    x = L0_attn_x
    xn = _layernorm(x, axis=-1)
    s = _L0_attn_ref(xn, L0_attn_q_w, L0_attn_q_b, L0_attn_k_w, L0_attn_k_b, L0_attn_v_w, L0_attn_v_b, L0_attn_o_w, L0_attn_o_b)
    g = _silu(_L0_ffn_ref(xn, L0_ffn_gate_w, L0_ffn_fc1_w, L0_ffn_fc1_b, L0_ffn_fc2_w, L0_ffn_fc2_b, L0_ffn_alpha))
    x = x + s * g
    return x

_drawn_inputs = setup_inputs


def setup_inputs(seed=0):
    import zlib

    import numpy as np

    out = dict(_drawn_inputs(seed))
    spreads = {'L0_ffn_fc1_b': (0.0, 0.8), 'L0_ffn_fc2_b': (0.0, 0.8)}
    factors = {'L0_attn_q_w': 8.0,
     'L0_attn_q_b': 8.0,
     'L0_attn_k_w': 8.0,
     'L0_attn_k_b': 8.0,
     'L0_attn_v_w': 8.0,
     'L0_attn_v_b': 8.0,
     'L0_attn_o_w': 8.0,
     'L0_attn_o_b': 8.0,
     'L0_ffn_gate_w': 8.0,
     'L0_ffn_fc1_w': 8.0,
     'L0_ffn_fc2_w': 8.0,
     'L0_ffn_alpha': 8.0}
    for name, (base, spread) in spreads.items():
        noise = np.random.default_rng([zlib.crc32(name.encode()), seed]).standard_normal(out[name].shape)
        drawn = base * np.exp(spread * noise) if base else spread * noise
        out[name] = jnp.asarray(drawn.astype(out[name].dtype))
    for name, factor in factors.items():
        out[name] = (out[name] * factor).astype(out[name].dtype)
    return out
```

```python
import concourse.bass as bass
from concourse import mybir
from contextlib import ExitStack

fp32 = mybir.dt.float32
bf16 = mybir.dt.bfloat16
ALU = mybir.AluOpType
ACT = mybir.ActivationFunctionType
AX = mybir.AxisListType

P = 128
B, T, D = 4, 1024, 256
H, HD = 16, 16
E = 8
KT = D // P
TB = T // P
NT = B * TB
HQ = 4
NQ = B * H // HQ
QF = HQ * HD
SCALE = HD ** -0.5
EPS = 1e-5
NEG = -3.0e38
BANK = 512

K_PART = (0, 0, 1, 1, 0, 2)
Q_PART = (0, 1, 0, 1, 2, 0)
NSPLIT = 3
DATA_ROWS = len(K_PART) * HD
DECAY_ROWS = (TB - 1) + 2
SCORE_ROWS = DATA_ROWS + DECAY_ROWS
ALL_ROWS = SCORE_ROWS + NSPLIT

PIECES = []
for ib in range(TB):
    for seg in range(0, P * (ib + 1), BANK):
        width = min(BANK, P * (ib + 1) - seg)
        heads = 4 if width == 128 else 2 if width == 256 else 1
        PIECES += [(ib, seg, width, h, heads) for h in range(0, HQ, heads)]
NP = len(PIECES)
TYPES = [[[(0, h, 0)] for h in range(HQ)]]
for jb in range(1, TB // 2):
    TYPES.append([[(jb, h, 0), (TB - jb, h, T - P * jb)] for h in range(HQ)])
TYPES.append([[(TB // 2, h, 0), (TB // 2, h + 1, T // 2)] for h in range(0, HQ, 2)])
NTY = len(TYPES)
UNITS = [(k, n, parts) for k, units in enumerate(TYPES) for n, parts in enumerate(units)]
NU = len(UNITS)
LAST_OF_TYPE = [sum(len(u) for u in TYPES[:k + 1]) for k in range(NTY)]
SPREAD = 16
PRO = NP + 1
WIN = NP + 1 + 2
CH = 512
NCH = B * T // CH
ARENA = 21 * 1024 + 640
YC = NCH + 1


def attention_moe_kernel(nc, x, wqT, wkT, wvT, woT, qb, kb, vb, ob, gate, w1, b1, w2, b2, alpha,
                         ident_f, ident_b, mask_neg, mask_negT, k_rows, q_rows, e_index, out):
    x_t = x.rearrange("b (t p) d -> p (b t) d", p=P)
    out_t = out.rearrange("b (t p) d -> p (b t) d", p=P)
    w1_t = w1.rearrange("e (k p) n -> p e k n", p=P)
    w2_t = w2.rearrange("e (k p) n -> p e k n", p=P)

    ctx = ExitStack()
    with ctx:
        def sb(name, shape, dt=fp32):
            return ctx.enter_context(nc.sbuf_tensor(name, shape, dt))

        def sem(name):
            return ctx.enter_context(nc.semaphore(name))

        k_parts = nc.dram_tensor("k_parts", [NSPLIT, NQ * QF, T], bf16).ap()
        q_parts = nc.dram_tensor("q_parts", [NSPLIT, NQ * QF, T], bf16).ap()

        wq_sb = sb("wq_sb", [P, KT, D])
        wk_sb = sb("wk_sb", [P, KT, D])
        wvg_sb = sb("wvg_sb", [P, KT, D + E])
        wo_sb = sb("wo_sb", [P, KT, D])
        qb_sb = sb("qb_sb", [P, KT])
        kb_sb = sb("kb_sb", [P, KT])
        kbs_sb = sb("kbs_sb", [P, KT])
        vb_sb = sb("vb_sb", [P, D])
        ob_sb = sb("ob_sb", [P, D])
        b1b = [sb(f"b1b{n}", [P, KT]) for n in range(2)]
        b2_sb = sb("b2_sb", [E, D])
        alpha_sb = sb("alpha_sb", [P, E])
        eidx_sb = sb("eidx_sb", [P, E])
        idf = sb("idf", [P, P])
        idb = sb("idb", [P, P], bf16)
        mask_sb = sb("mask_sb", [P, P], bf16)
        maskT_sb = sb("maskT_sb", [P, P], bf16)
        xnT_all = sb("xnT_all", [P, KT, B * T])
        v_all = sb("v_all", [P, NQ, TB, QF])
        logits = sb("logits", [P, NT, E])
        comb = sb("comb", [P, NT, E])
        arena = sb("arena", [P, ARENA])

        at = [0]

        def cut(cols, dt=fp32):
            words = cols if dt == fp32 else cols // 2
            a = arena[:, at[0]:at[0] + words]
            at[0] += words
            assert at[0] <= ARENA
            return a if dt == fp32 else a.bitcast(dt)

        xb = cut(TB * D).rearrange("p (t d) -> p t d", d=D)
        xnb = cut(TB * D).rearrange("p (t d) -> p t d", d=D)
        xnT_b = cut(KT * T).rearrange("p (k t) -> p k t", k=KT)
        whole = [cut(T) for _ in range(4)]
        parts = [cut(NSPLIT * T, bf16).rearrange("p (s t) -> p s t", s=NSPLIT) for _ in range(4)]
        at[0] = 0
        probs = [cut(T) for _ in range(2 * HQ)]
        a_all = cut(NQ * TB * QF).rearrange("p (q t f) -> p q t f", q=NQ, t=TB)
        oT = cut(T)
        gat = [cut(NT * E).rearrange("p (t e) -> p t e", e=E) for _ in range(4)]
        col = [cut(NT) for _ in range(8)]
        at[0] = 8 * T + NQ * TB * QF
        w1b = [cut(KT * D).rearrange("p (k n) -> p k n", k=KT) for _ in range(2)]
        w2b = [cut(KT * D).rearrange("p (k n) -> p k n", k=KT) for _ in range(2)]
        gT = [cut(KT * CH).rearrange("p (k t) -> p k t", k=KT) for _ in range(2)]
        at[0] = 0
        acc = cut(NT * D).rearrange("p (t d) -> p t d", d=D)
        at[0] = 8 * T + NQ * TB * QF
        xo = [cut(2 * D) for _ in range(2)]
        aT = [cut(2 * D) for _ in range(2)]
        a_tok = [cut(2 * D) for _ in range(2)]
        c_tok = [cut(2 * E).rearrange("p (t e) -> p t e", e=E) for _ in range(2)]
        gsum = [cut(2 * D) for _ in range(2)]
        so = [cut(2 * D) for _ in range(2)]
        cT = [cut(2 * P)[0:E, :] for _ in range(2)]

        k_aug = [sb(f"k_aug{n}", [P, HQ, T], bf16) for n in range(2)]
        q_aug = [sb(f"q_aug{n}", [P, HQ, T], bf16) for n in range(2)]
        v_q = [sb(f"v_q{n}", [P, TB, HQ, 2 * HD]) for n in range(2)]
        mxa = sb("mxa", [P, HQ, TB])
        mxb = sb("mxb", [P, HQ, TB // 2])
        mrest = sb("mrest", [P, HQ, TB])
        msplit = sb("msplit", [P, NSPLIT * TB * HQ], bf16)
        mT = sb("mT", [NSPLIT * TB * HQ, P], bf16)
        rden = [sb(f"rden{n}", [P, TB // 2, HQ]) for n in range(2)]
        stats = sb("stats", [P, TB, 6])
        mv = sb("mv", [P, TB, 2])
        veps = sb("veps", [P, TB])
        std = sb("std", [P, TB])
        rstd = sb("rstd", [P, TB])

        ps = ctx.enter_context(nc.psum_tensor("ps", [P, 8 * BANK], fp32))

        def bank(n, k=1):
            return ps[:, n * BANK:(n + k) * BANK]

        consts_in = sem("consts_in")
        bias_ready = sem("bias_ready"); ln_step = sem("ln_step"); split_step = sem("split_step")
        gate_step = sem("gate_step"); m_step = sem("m_step"); o_step = sem("o_step"); fin_step = sem("fin_step")
        x_in = sem("x_in"); xb_free = sem("xb_free")
        var_ready = sem("var_ready"); std_ready = sem("std_ready"); xn_ready = sem("xn_ready")
        xpose_done = sem("xpose_done"); xT_ready = sem("xT_ready"); xT_kept = sem("xT_kept")
        proj_done = sem("proj_done"); proj_out = sem("proj_out"); split_done = sem("split_done")
        parts_out = sem("parts_out")
        v_done = sem("v_done"); v_out = sem("v_out")
        gap_ready = sem("gap_ready"); gexp_ready = sem("gexp_ready")
        ones_set = sem("ones_set"); vq_ready = sem("vq_ready")
        aug_in = sem("aug_in"); piece_done = sem("piece_done"); piece_used = sem("piece_used")
        m_split = sem("m_split"); mT_ready = sem("mT_ready"); m_in = sem("m_in")
        s_done = sem("s_done"); exp_done = sem("exp_done");
        pv_done = sem("pv_done"); o_out = sem("o_out")
        acc_zero = sem("acc_zero"); w_in = [sem(f"w_in{n}") for n in range(2)]
        h_done = sem("h_done"); g_done = sem("g_done"); y_done = sem("y_done"); acc_done = sem("acc_done")
        xo_in = [sem(f"xo_in{n}") for n in range(2)]; at_done = sem("at_done"); at_out = sem("at_out"); sg_done = sem("sg_done")
        gsum_done = sem("gsum_done"); silu_done = sem("silu_done"); fin_done = sem("fin_done")
        passed = sem("passed")
        stored = [sem(f"stored{n}") for n in range(2)]; sg_used = sem("sg_used"); tok_ready = sem("tok_ready")

        NCONST = 16 + 4
        CONSTS = 16 * NCONST
        SIDES = [(side, m) for side in range(2) for m in range(KT)]
        PROJ = [(n, c) for n in range(4) for c in range(T // BANK)]

        block = ctx.enter_context(nc.Block())

        @block.sync
        def _(sp):
            sp.sem_inc(parts_out, 16 * 4)
            for par in range(2):
                sp.sem_inc(stored[par], 16)
            for dst, src in ((idf[:, :], ident_f), (wq_sb, wqT.rearrange("(k p) n -> p k n", p=P)),
                             (wk_sb, wkT.rearrange("(k p) n -> p k n", p=P)),
                             (wvg_sb[:, :, 0:D], wvT.rearrange("(k p) n -> p k n", p=P)),
                             (wvg_sb[:, :, D:D + E], gate.rearrange("(k p) n -> p k n", p=P)),
                             (wo_sb, woT.rearrange("(k p) n -> p k n", p=P)),
                             (qb_sb, qb), (kb_sb, kb), (vb_sb, vb), (ob_sb, ob),
                             (b2_sb, b2), (alpha_sb, alpha), (eidx_sb, e_index),
                             (idb, ident_b), (mask_sb, mask_neg), (maskT_sb, mask_negT)):
                dst = dst if isinstance(dst, bass.AP) else dst[tuple(slice(None) for _ in dst.shape)]
                sp.dma_start(dst, src).then_inc(consts_in, 16)
            for par in range(2):
                sp.dma_start(k_aug[par][DATA_ROWS:SCORE_ROWS], k_rows).then_inc(consts_in, 16)
                sp.dma_start(q_aug[par][DATA_ROWS:ALL_ROWS], q_rows).then_inc(consts_in, 16)

            with sp.Fori(0, B) as b:
                sp.wait_ge(xb_free, b + 1)
                sp.dma_start(xb, x_t[:, bass.ts(b, TB), :]).then_inc(x_in, 16)
                for n, (side, m) in enumerate(SIDES):
                    sp.wait_ge(split_done, 4 * b + n + 5)
                    dst = (k_parts, q_parts)[side]
                    sp.dma_start(dst[:, bass.ds(b * D + m * P, P), :].rearrange("s p t -> p s t"),
                                 parts[n]).then_inc(parts_out, 16)

            def load_quad(q, par):
                for g in range(len(K_PART)):
                    rows = slice(HD * g, HD * (g + 1))
                    for aug, src, part in ((k_aug, k_parts, K_PART[g]), (q_aug, q_parts, Q_PART[g])):
                        sp.dma_start(aug[par][rows, :, :],
                                     src[part, bass.ts(q, QF), :].rearrange("(h d) t -> d h t", d=HD)
                                     ).then_inc(aug_in, 16)

            def load_maxima(q, par):
                sp.wait_ge(mT_ready, q + 1)
                for s in range(NSPLIT):
                    dst = k_aug[par][SCORE_ROWS + s:SCORE_ROWS + s + 1, :, :]
                    rows = mT[s * TB * HQ:(s + 1) * TB * HQ, :]
                    sp.dma_start(dst.rearrange("o h (t i) -> o (h t) i", t=TB),
                                 rows).then_inc(m_in, 16)

            sp.wait_ge(parts_out, 16 * 4 * (B + 1))
            load_quad(0, 0)
            load_maxima(0, 0)

            def window(q, par, last):
                if not last:
                    sp.wait_ge(s_done, NU * q + 1)
                    load_quad(q + 1, 1 - par)
                    load_maxima(q + 1, 1 - par)

            with sp.Fori(0, NQ // 2 - 1) as t:
                for par in range(2):
                    window(2 * t + par, par, False)
            for par in range(2):
                window(NQ - 2 + par, par, par == 1)

            sp.wait_ge(acc_zero, 1)
            with sp.Fori(0, E // 2) as t:
                for par in range(2):
                    e = 2 * t + par
                    sp.wait_ge(y_done, NCH * e + 1)
                    sp.dma_start(w1b[par], w1_t[:, e, :, :]).then_inc(w_in[par], 16)
                    sp.dma_start(w2b[par], w2_t[:, e, :, :]).then_inc(w_in[par], 16)
                    sp.dma_start(b1b[par][:, :], b1[e, :, :]).then_inc(w_in[par], 16)

            sp.wait_ge(acc_done, NCH * E + 2)
            with sp.Fori(0, NT // 4) as t:
                for par in range(2):
                    sp.wait_ge(stored[par], 16 * t + 16)
                    sp.dma_start(xo[par].rearrange("p (t d) -> p t d", d=D),
                                 x_t[:, bass.ts(2 * t + par, 2), :]).then_inc(xo_in[par], 16)
                for par in range(2):
                    n = 2 * t + par
                    sp.wait_ge(fin_done, n + 1)
                    sp.dma_start(out_t[:, bass.ts(n, 2), :],
                                 xo[par].rearrange("p (t d) -> p t d", d=D)).then_inc(stored[par], 16)
            for par in range(2):
                sp.wait_ge(stored[par], 16 * (NT // 4) + 16)

        @block.gpsimd
        def _(pool):
            pool.sem_inc(xT_kept, 1)
            for par in range(2):
                pool.memset(v_q[par][:, :, :, HD:2 * HD], 1.0).then_inc(ones_set, 1)
            with pool.Fori(0, B) as b:
                pool.wait_ge(xT_ready, 4 * b + 8)
                nc.gpsimd.tensor_copy(xnT_all[:, :, bass.ts(b, T)], xnT_b).then_inc(xT_kept, 1)

            def take_v(q, par):
                nc.gpsimd.tensor_copy(v_q[par][:, :, :, 0:HD],
                                      v_all[:, q, :, :].rearrange("p t (h d) -> p t h d", d=HD)
                                      ).then_inc(vq_ready, 1)

            pool.wait_ge(v_out, NT + 2)
            take_v(0, 0)

            def next_v(q, par):
                pool.wait_ge(pv_done, NTY * q + 2)
                take_v(q + 1, 1 - par)

            with pool.Fori(0, NQ // 2 - 1) as t:
                for par in range(2):
                    next_v(2 * t + par, par)
            next_v(NQ - 2, 0)
            pool.wait_ge(piece_used, PRO + WIN * (NQ - 1) + 4)
            nc.gpsimd.memset(acc, 0.0).then_inc(acc_zero, 1)
            pool.wait_ge(acc_done, NCH * E + 2)
            with pool.Fori(0, NT // 4) as t:
                for par in range(2):
                    n = 2 * t + par
                    pool.wait_ge(at_done, n + 1)
                    b, i = n // (TB // 2), n % (TB // 2)
                    nc.gpsimd.tensor_copy(a_tok[par].rearrange("p (t q f) -> p q t f", t=2, f=QF),
                                          a_all[:, bass.ts(b, HQ), bass.ts(i, 2), :])
                    nc.gpsimd.tensor_copy(c_tok[par], comb[:, bass.ts(n, 2), :]).then_inc(tok_ready, 1)

        @block.scalar
        def _(act):
            act.sem_inc(xT_ready, 4)
            act.sem_inc(proj_out, 2)
            act.sem_inc(exp_done, 2)
            act.sem_inc(o_out, 1)
            act.sem_inc(g_done, 2)
            act.sem_inc(at_out, 2)
            act.sem_inc(silu_done, 2)
            act.wait_ge(consts_in, CONSTS)
            with act.Fori(0, B) as b:
                act.wait_ge(var_ready, b + 1)
                nc.scalar.activation(std[:, :], veps[:, :], ACT.Sqrt).then_inc(std_ready, 1)
                act.wait_ge(xT_kept, b + 1)
                for n in range(4):
                    act.wait_ge(xpose_done, 4 * b + n + 5)
                    k, half = divmod(n, 2)
                    nc.scalar.activation(xnT_b[:, k, half * BANK:(half + 1) * BANK], bank(n),
                                         ACT.Copy).then_inc(xT_ready, 1)
                act.wait_ge(parts_out, 64 * b + 64)
                for i, (n, c) in enumerate(PROJ):
                    side, m = SIDES[n]
                    act.wait_ge(proj_done, 8 * b + i + 1)
                    if c == 0:
                        act.wait_ge(split_done, 4 * b + n + 1)
                    cs = slice(c * BANK, (c + 1) * BANK)
                    bias = (kbs_sb, qb_sb)[side][:, m:m + 1]
                    scale = (SCALE, 1.0)[side]
                    nc.scalar.activation(whole[n][:, cs], bank(4 + i % 2), ACT.Identity, bias=bias, scale=scale)
                    nc.scalar.activation(parts[n][:, 0, cs], bank(4 + i % 2), ACT.Identity, bias=bias,
                                         scale=scale).then_inc(proj_out, 1)
            act.wait_ge(xT_kept, B + 1)
            act.wait_ge(gap_ready, 1)
            nc.scalar.activation(col[4][:, :], col[3][:, :], ACT.Exp).then_inc(gexp_ready, 1)

            def window(q, par):
                for n, (k, u, unit) in enumerate(UNITS):
                    if u == 0:
                        act.wait_ge(pv_done, NTY * q + k + 1)
                    act.wait_ge(s_done, NU * q + n + 2)
                    nc.scalar.activation(probs[HQ * ((par + k) % 2) + u], bank(2 + 2 * (n % 2), 2),
                                         ACT.Exp).then_inc(exp_done, 1)
                act.wait_ge(pv_done, NTY * q + NTY + 2)
                nc.scalar.activation(oT, bank(6, 2), ACT.Copy).then_inc(o_out, 1)

            with act.Fori(0, NQ // 2 - 1) as t:
                for par in range(2):
                    window(2 * t + par, par)
            for par in range(2):
                window(NQ - 2 + par, par)

            with act.Fori(0, E // 2) as t:
                for par in range(2):
                    e = 2 * t + par
                    for c in range(NCH):
                        act.wait_ge(h_done, NCH * e + c + 1)
                        act.wait_ge(y_done, NCH * e + c + YC - 1)
                        for m in range(KT):
                            ins = nc.scalar.activation(gT[c % 2][:, m, :], bank(2 * (c % 2) + m), ACT.Gelu,
                                                       bias=b1b[par][:, m:m + 1])
                        ins.then_inc(g_done, 1)

            with act.Fori(0, NT // 4) as t:
                for par in range(2):
                    n = 2 * t + par
                    act.wait_ge(at_done, n + 3)
                    nc.scalar.activation(aT[par], bank(4 * par), ACT.Copy)
                    nc.scalar.activation(cT[par], bank(4 * par + 1)[0:E, 0:2 * P], ACT.Copy).then_inc(at_out, 1)
                    act.wait_ge(gsum_done, n + 1)
                    nc.scalar.activation(gsum[par], gsum[par], ACT.Silu).then_inc(silu_done, 1)

        @block.vector
        def _(dve):
            def spread(ap, n):
                return bass.AP(ap.tensor, ap.offset, [list(x) for x in ap.ap] + [[0, n]])

            def over_tiles(ap, n):
                return bass.AP(ap.tensor, ap.offset, [list(ap.ap[0]), [0, n]] + [list(x) for x in ap.ap[1:]])

            dve.sem_inc(xb_free, 1)
            dve.sem_inc(split_done, 4)
            dve.sem_inc(v_out, 2)
            dve.sem_inc(piece_used, 2)
            dve.sem_inc(acc_done, 2)
            dve.sem_inc(sg_used, 2)
            dve.wait_ge(consts_in, CONSTS)
            nc.vector.tensor_scalar(kbs_sb[:, :], kb_sb[:, :], SCALE, None, ALU.mult).then_inc(bias_ready, 1)
            with dve.Fori(0, B) as b:
                dve.wait_ge(x_in, 16 * b + 16)
                for t in range(TB):
                    ins = nc.vector.bn_stats(stats[:, t, :], xb[:, t, :])
                ins.then_inc(ln_step, 1)
                dve.wait_ge(ln_step, 3 * b + 1)
                dve.sem_inc(passed, 1)
                for t in range(TB):
                    ins = nc.vector.bn_aggr(mv[:, t, :], stats[:, t, :])
                ins.then_inc(ln_step, 1)
                dve.wait_ge(ln_step, 3 * b + 2)
                nc.vector.tensor_scalar(veps[:, :], mv[:, :, 1], EPS, None, ALU.add).then_inc(var_ready, 1)
                dve.wait_ge(std_ready, b + 1)
                nc.vector.reciprocal(rstd[:, :], std[:, :]).then_inc(ln_step, 1)
                dve.wait_ge(ln_step, 3 * b + 3)
                dve.wait_ge(xpose_done, 4 * b + 4)
                for t in range(TB):
                    ins = nc.vector.tensor_scalar(xnb[:, t, :], xb[:, t, :], mv[:, t, 0:1], rstd[:, t:t + 1],
                                                  ALU.subtract, ALU.mult)
                ins.then_inc(xn_ready, 1)
                dve.wait_ge(xn_ready, b + 1)
                dve.sem_inc(xb_free, 1)
                for n in range(4):
                    dve.wait_ge(proj_out, 8 * b + 2 * n + 4)
                    nc.vector.tensor_tensor(whole[n], whole[n], parts[n][:, 0, :],
                                            ALU.subtract).then_inc(split_step, 1)
                    dve.wait_ge(split_step, 8 * b + 2 * n + 1)
                    nc.vector.tensor_copy(parts[n][:, 1, :], whole[n]).then_inc(split_step, 1)
                    dve.wait_ge(split_step, 8 * b + 2 * n + 2)
                    nc.vector.tensor_tensor(parts[n][:, 2, :], whole[n], parts[n][:, 1, :],
                                            ALU.subtract).then_inc(split_done, 1)
                for t in range(TB):
                    dve.wait_ge(v_done, TB * b + t + 1)
                    vp = bank(6 + t % 2)
                    nc.vector.tensor_tensor(v_all[:, bass.ts(b, HQ), t, :],
                                            vp[:, 0:D].rearrange("p (g f) -> p g f", f=QF),
                                            vb_sb[:, :].rearrange("p (g f) -> p g f", f=QF), ALU.add)
                    nc.vector.tensor_copy(logits[:, TB * b + t, :], vp[:, D:D + E]).then_inc(v_out, 1)

            def reduce_piece(i, piece):
                ib, seg, width, h, heads = piece
                src = bank(i % 2)[:, 0:width * heads].rearrange("p (h j) -> p h j", h=heads)
                dst = mxb[:, h:h + heads, ib - TB // 2] if seg else mxa[:, h:h + heads, ib]
                return nc.vector.tensor_reduce(dst, src, AX.X, ALU.max)

            def split_maxima(q):
                dst = [msplit[:, s * TB * HQ:(s + 1) * TB * HQ].rearrange("p (h t) -> p h t", t=TB)
                       for s in range(NSPLIT)]
                nc.vector.tensor_tensor(mxa[:, :, TB // 2:TB], mxa[:, :, TB // 2:TB], mxb[:, :, :],
                                        ALU.max).then_inc(m_step, 1)
                dve.wait_ge(m_step, 4 * q + 1)
                nc.vector.tensor_copy(dst[0], mxa[:, :, :]).then_inc(m_step, 1)
                dve.wait_ge(m_step, 4 * q + 2)
                nc.vector.tensor_tensor(mrest[:, :, :], mxa[:, :, :], dst[0], ALU.subtract).then_inc(m_step, 1)
                dve.wait_ge(m_step, 4 * q + 3)
                nc.vector.tensor_copy(dst[1], mrest[:, :, :]).then_inc(m_step, 1)
                dve.wait_ge(m_step, 4 * q + 4)
                nc.vector.tensor_tensor(dst[2], mrest[:, :, :], dst[1], ALU.subtract).then_inc(m_split, 1)

            def maxima(q, base, odd):
                for i, piece in enumerate(PIECES):
                    dve.wait_ge(piece_done, base + i + 1)
                    reduce_piece(odd + i, piece).then_inc(piece_used, 1)
                dve.wait_ge(piece_used, base + NP + 2)
                split_maxima(q)
                dve.wait_ge(piece_done, base + NP + 1)
                return nc.vector.tensor_copy(mT[:, :], bank((odd + NP) % 2).bitcast(bf16)[0:NSPLIT * TB * HQ, 0:P])

            def maxima_out(ins):
                ins.then_inc(mT_ready, 1)

            maxima_out(maxima(0, 0, 0))
            dve.wait_ge(mT_ready, 1)
            dve.sem_inc(piece_used, 1)

            step = [0]

            def after(ins):
                step[0] += 1
                ins.then_inc(gate_step, 1)
                dve.wait_ge(gate_step, step[0])

            dve.wait_ge(v_out, NT + 2)
            index = over_tiles(eidx_sb[:, :], NT)
            best, first, second, gap, gexp, place, norm, low = col

            def choose(values, top, where, chosen):
                after(nc.vector.tensor_reduce(top, values, AX.X, ALU.max))
                after(nc.vector.tensor_tensor(gat[0], values, spread(top, E), ALU.is_lt))
                after(nc.vector.scalar_tensor_tensor(gat[0], gat[0], float(E), index, ALU.mult, ALU.add))
                after(nc.vector.tensor_reduce(where, gat[0], AX.X, ALU.min))
                after(nc.vector.tensor_tensor(chosen, index, spread(where, E), ALU.is_equal))

            choose(logits[:, :, :], best, place, gat[1])
            after(nc.vector.scalar_tensor_tensor(gat[2], gat[1], NEG, logits[:, :, :], ALU.mult, ALU.add))
            choose(gat[2], second, place, gat[3])
            nc.vector.tensor_tensor(gap, second, best, ALU.subtract).then_inc(gap_ready, 1)
            dve.wait_ge(gexp_ready, 1)
            after(nc.vector.tensor_scalar(norm, gexp, 1.0, None, ALU.add))
            after(nc.vector.reciprocal(first, norm))
            after(nc.vector.tensor_tensor(low, gexp, first, ALU.mult))
            after(nc.vector.tensor_tensor(gat[1], gat[1], spread(first, E), ALU.mult))
            after(nc.vector.tensor_tensor(gat[3], gat[3], spread(low, E), ALU.mult))
            after(nc.vector.tensor_tensor(gat[1], gat[1], gat[3], ALU.add))
            after(nc.vector.tensor_tensor(comb[:, :, :], gat[1], over_tiles(alpha_sb[:, :], NT), ALU.mult))

            def window(q, par, last):
                base, odd = PRO + WIN * q, 1 + par
                if not last:
                    ins = maxima(q + 1, base, odd)
                    ins.then_inc(mT_ready, 1)
                    dve.wait_ge(mT_ready, q + 2)
                    dve.sem_inc(piece_used, 1)
                    base, odd = base + NP + 1, odd + NP + 1
                for half in range(2):
                    dve.wait_ge(piece_done, base + half + 1)
                    o = bank((odd + half) % 2).rearrange("p (t h c) -> p t h c", t=TB // 2, h=HQ)
                    nc.vector.reciprocal(rden[half][:, :, :], o[:, :, :, HD]).then_inc(o_step, 1)
                    dve.wait_ge(o_step, 2 * q + half + 1)
                    dst = a_all[:, q, half * TB // 2:(half + 1) * TB // 2, :]
                    nc.vector.tensor_tensor(dst.rearrange("p t (h d) -> p t h d", d=HD), o[:, :, :, 0:HD],
                                            spread(rden[half][:, :, :], HD), ALU.mult).then_inc(piece_used, 1)

            with dve.Fori(0, NQ // 2 - 1) as t:
                for par in range(2):
                    window(2 * t + par, par, False)
            for par in range(2):
                window(NQ - 2 + par, par, par == 1)

            dve.wait_ge(acc_zero, 1)
            with dve.Fori(0, E // 2) as t:
                for par in range(2):
                    e = 2 * t + par
                    for c in range(NCH):
                        dve.wait_ge(y_done, NCH * e + c + 1 + YC)
                        for j in range(CH // P):
                            tile = c * (CH // P) + j
                            y = bank(4 + 2 * (c % 2) + j // 2)[:, (j % 2) * D:(j % 2 + 1) * D]
                            ins = nc.vector.scalar_tensor_tensor(acc[:, tile, :], y, comb[:, tile, bass.ds(e, 1)],
                                                                 acc[:, tile, :], ALU.mult, ALU.add)
                        ins.then_inc(acc_done, 1)

            ob2 = over_tiles(ob_sb[:, :], 2)
            dve.wait_ge(acc_done, NCH * E + 2)
            with dve.Fori(0, NT // 4) as t:
                for par in range(2):
                    n = 2 * t + par
                    dve.wait_ge(sg_done, n + 1)
                    dve.wait_ge(silu_done, n + 1)
                    nc.vector.tensor_tensor(gsum[par], acc[:, bass.ts(n, 2), :].rearrange("p t d -> p (t d)"),
                                            bank(4 * par + 3), ALU.add).then_inc(gsum_done, 1)
                    nc.vector.tensor_tensor(so[par].rearrange("p (t d) -> p t d", d=D),
                                            bank(4 * par + 2).rearrange("p (t d) -> p t d", d=D), ob2,
                                            ALU.add).then_inc(sg_used, 1)
                    dve.wait_ge(sg_used, n + 3)
                    dve.wait_ge(silu_done, n + 3)
                    nc.vector.tensor_tensor(so[par], so[par], gsum[par], ALU.mult).then_inc(fin_step, 1)
                    dve.wait_ge(fin_step, n + 1)
                    dve.wait_ge(xo_in[par], 16 * t + 16)
                    nc.vector.tensor_tensor(xo[par], xo[par], so[par], ALU.add).then_inc(fin_done, 1)

        @block.tensor
        def _(pe):
            pe.sem_inc(xpose_done, 4)
            pe.sem_inc(s_done, 1)
            pe.sem_inc(pv_done, 2)
            pe.sem_inc(y_done, YC)
            pe.sem_inc(at_done, 2)
            pe.wait_ge(consts_in, CONSTS)
            with pe.Fori(0, B) as b:
                pe.wait_ge(xn_ready, b + 1)
                pe.wait_ge(xT_ready, 4 * b + 4)
                for n in range(4):
                    k, half = divmod(n, 2)
                    for j in range(BANK // P):
                        ins = nc.tensor.transpose(bank(n)[:, j * P:(j + 1) * P],
                                                  xnb[:, half * (BANK // P) + j, k * P:(k + 1) * P], idf[:, :])
                    ins.then_inc(xpose_done, 1)
                pe.wait_ge(xT_ready, 4 * b + 8)
                for i, (n, c) in enumerate(PROJ):
                    side, m = SIDES[n]
                    pe.wait_ge(proj_out, 8 * b + i + 1)
                    for k in range(KT):
                        ins = nc.tensor.matmul(bank(4 + i % 2), (wk_sb, wq_sb)[side][:, k, m * P:(m + 1) * P],
                                               xnT_b[:, k, c * BANK:(c + 1) * BANK],
                                               start=(k == 0), stop=(k == KT - 1))
                    ins.then_inc(proj_done, 1)
                for t in range(TB):
                    pe.wait_ge(v_out, TB * b + t + 1)
                    for k in range(KT):
                        ins = nc.tensor.matmul(bank(6 + t % 2)[:, 0:D + E], xnT_b[:, k, t * P:(t + 1) * P],
                                               wvg_sb[:, k, :], start=(k == 0), stop=(k == KT - 1))
                    ins.then_inc(v_done, 1)

            def score_piece(i, par, piece):
                ib, seg, width, h0, heads = piece
                diagonal = seg + width == P * (ib + 1)
                for n in range(heads):
                    out_ = bank(i % 2)[:, n * width:(n + 1) * width]
                    ins = nc.tensor.matmul(out_, k_aug[par][0:SCORE_ROWS, h0 + n, ib * P:(ib + 1) * P],
                                           q_aug[par][0:SCORE_ROWS, h0 + n, seg:seg + width],
                                           start=True, stop=not diagonal)
                    if diagonal:
                        ins = nc.tensor.matmul(out_[:, width - P:width], idb[:, :], mask_sb[:, :],
                                               start=False, stop=True)
                return ins

            def send_piece(base, i, odd, par):
                pe.wait_ge(piece_used, base + i + 1)
                score_piece(odd + i, par, PIECES[i]).then_inc(piece_done, 1)

            def send_maxima(q, base, odd):
                pe.wait_ge(m_split, q + 1)
                pe.wait_ge(piece_used, base + NP + 1)
                nc.tensor.transpose(bank((odd + NP) % 2).bitcast(bf16)[0:NSPLIT * TB * HQ, 0:P], msplit[:, :],
                                    idb[:, :]).then_inc(piece_done, 1)

            def unit_scores(par, n, unit):
                base = (2 + 2 * (n % 2)) * BANK
                for jb, h, col0 in unit:
                    columns = q_aug[par][0:ALL_ROWS, h, jb * P:(jb + 1) * P]
                    lo, i0 = col0, P * jb
                    end = col0 + T - P * jb
                    while lo < end:
                        hi = min(end, (lo // BANK + 1) * BANK)
                        ins = nc.tensor.matmul(ps[:, base + lo:base + hi], columns,
                                               k_aug[par][0:ALL_ROWS, h, i0:i0 + hi - lo],
                                               start=True, stop=lo > col0)
                        if lo == col0:
                            ins = nc.tensor.matmul(ps[:, base + lo:base + lo + P], idb[:, :], maskT_sb[:, :],
                                                   start=False, stop=True)
                        i0 += hi - lo
                        lo = hi
                return ins

            def type_outputs(par, k):
                work = {}
                for u, unit in enumerate(TYPES[k]):
                    slot = probs[HQ * ((par + k) % 2) + u]
                    for jb, h, col0 in unit:
                        for c in range(2):
                            lo = max(P * jb, c * BANK)
                            if lo < (c + 1) * BANK:
                                at_ = col0 + lo - P * jb
                                work.setdefault((jb, c), []).append(
                                    (h, lo, (c + 1) * BANK, slot[:, at_:at_ + (c + 1) * BANK - lo]))
                for (jb, c), heads in work.items():
                    last = jb == TB // 2 - 1 if c == 0 else jb == TB // 2
                    for h, lo, hi, p in heads:
                        ins = nc.tensor.matmul(ps[2 * HD * h:2 * HD * (h + 1), 6 * BANK + lo:6 * BANK + hi],
                                               v_q[par][:, jb, h, :], p, start=(jb == 0), stop=last)
                return ins

            pe.wait_ge(aug_in, 16 * 12)
            for i in range(NP):
                send_piece(0, i, 0, 0)
            send_maxima(0, 0, 0)
            pe.wait_ge(ones_set, 2)

            def window(q, par, last):
                base, odd = PRO + WIN * q, 1 + par
                sent = 0
                pe.wait_ge(m_in, 48 * q + 48)
                for n, (k, u, unit) in enumerate(UNITS):
                    pe.wait_ge(exp_done, NU * q + n + 1)
                    unit_scores(par, n, unit).then_inc(s_done, 1)
                    if not last:
                        if n == 0:
                            pe.wait_ge(aug_in, 192 * q + 2 * 192)
                        upto = min(NP, -(-NP * (n + 1) // SPREAD))
                        for i in range(sent, upto):
                            send_piece(base, i, odd, 1 - par)
                        sent = upto
                    if u == 1 and k > 0 or n == NU - 1:
                        for kk in ([k - 1] if n < NU - 1 else [k - 1, k]):
                            if kk == 0:
                                pe.wait_ge(vq_ready, q + 1)
                                pe.wait_ge(o_out, q + 1)
                            pe.wait_ge(exp_done, NU * q + LAST_OF_TYPE[kk] + 2)
                            type_outputs(par, kk).then_inc(pv_done, 1)
                if not last:
                    send_maxima(q + 1, base, odd)
                    base, odd = base + NP + 1, odd + NP + 1
                pe.wait_ge(o_out, q + 2)
                for half in range(2):
                    pe.wait_ge(piece_used, base + half + 1)
                    for j in range(TB // 2):
                        i = half * TB // 2 + j
                        ins = nc.tensor.transpose(bank((odd + half) % 2)[:, j * P:(j + 1) * P],
                                                  oT[:, i * P:(i + 1) * P], idf[:, :])
                    ins.then_inc(piece_done, 1)

            with pe.Fori(0, NQ // 2 - 1) as t:
                for par in range(2):
                    window(2 * t + par, par, False)
            for par in range(2):
                window(NQ - 2 + par, par, par == 1)

            pe.wait_ge(piece_used, PRO + WIN * (NQ - 1) + 4)

            def hidden(e, par, c):
                pe.wait_ge(g_done, NCH * e + c + 1)
                for m in range(KT):
                    for k in range(KT):
                        ins = nc.tensor.matmul(bank(2 * (c % 2) + m), w1b[par][:, k, m * P:(m + 1) * P],
                                               xnT_all[:, k, c * CH:(c + 1) * CH],
                                               start=(k == 0), stop=(k == KT - 1))
                ins.then_inc(h_done, 1)

            def expert_out(e, par, c):
                pe.wait_ge(g_done, NCH * e + c + 3)
                pe.wait_ge(acc_done, NCH * e + c + 1)
                for j in range(CH // P):
                    for m in range(KT):
                        ins = nc.tensor.matmul(bank(4 + 2 * (c % 2) + j // 2)[:, (j % 2) * D:(j % 2 + 1) * D],
                                               gT[c % 2][:, m, j * P:(j + 1) * P], w2b[par][:, m, :],
                                               start=(m == 0), stop=(m == KT - 1))
                ins.then_inc(y_done, 1)

            with pe.Fori(0, E // 2) as t:
                for par in range(2):
                    e = 2 * t + par
                    pe.wait_ge(w_in[par], 48 * t + 48)
                    hidden(e, par, 0)
                    for c in range(1, NCH):
                        hidden(e, par, c)
                        expert_out(e, par, c - 1)
                    expert_out(e, par, NCH - 1)

            pe.wait_ge(acc_done, NCH * E + 2)
            with pe.Fori(0, NT // 4) as t:
                for par in range(2):
                    n = 2 * t + par
                    pe.wait_ge(tok_ready, n + 1)
                    pe.wait_ge(at_out, n + 1)
                    for j in range(2):
                        for k in range(KT):
                            s = j * KT + k
                            nc.tensor.transpose(bank(4 * par)[:, s * P:(s + 1) * P],
                                                a_tok[par][:, s * P:(s + 1) * P], idf[:, :])
                        ins = nc.tensor.transpose(bank(4 * par + 1)[0:E, j * P:(j + 1) * P], c_tok[par][:, j, :],
                                                  idf[:, :])
                    ins.then_inc(at_done, 1)
                    pe.wait_ge(at_out, n + 3)
                    pe.wait_ge(sg_used, n + 1)
                    for j in range(2):
                        cols = slice(j * D, (j + 1) * D)
                        for k in range(KT):
                            s = j * KT + k
                            nc.tensor.matmul(bank(4 * par + 2)[:, cols], aT[par][:, s * P:(s + 1) * P], wo_sb[:, k, :],
                                             start=(k == 0), stop=(k == KT - 1))
                        ins = nc.tensor.matmul(bank(4 * par + 3)[:, cols], cT[par][:, j * P:(j + 1) * P], b2_sb[:, :],
                                               start=True, stop=True)
                    ins.then_inc(sg_done, 1)


def kernel(**inputs):
    import numpy as np
    import concourse.bacc as bacc
    from concourse.bass_utils import run_bass_kernel_spmd

    def rows(n, m):
        return np.ascontiguousarray(np.broadcast_to(n, (m,) + n.shape))

    def block_(name):
        return np.asarray(inputs[name])

    bf = mybir.dt.np(bf16)
    pos = np.arange(T)
    tile, within = pos // P, pos % P
    border = np.arange(1, TB)[:, None]
    k_rows = np.concatenate([(tile[None] >= border).astype(np.float32), -within[None], np.ones((1, T))])
    q_rows = np.concatenate([-P * (tile[None] < border).astype(np.float32), np.ones((1, T)), within[None],
                             -np.ones((NSPLIT, T))])
    heads = lambda a: np.ascontiguousarray(np.broadcast_to(a[:, None, :], (a.shape[0], HQ, T))).astype(bf)
    low = np.tril(np.ones((P, P), bool))
    args = {
        "x": block_("L0_attn_x"),
        "wqT": np.ascontiguousarray(block_("L0_attn_q_w").T),
        "wkT": np.ascontiguousarray(block_("L0_attn_k_w").T),
        "wvT": np.ascontiguousarray(block_("L0_attn_v_w").T),
        "woT": np.ascontiguousarray(block_("L0_attn_o_w").T),
        "qb": np.ascontiguousarray(block_("L0_attn_q_b").reshape(KT, P).T),
        "kb": np.ascontiguousarray(block_("L0_attn_k_b").reshape(KT, P).T),
        "vb": rows(block_("L0_attn_v_b"), P),
        "ob": rows(block_("L0_attn_o_b"), P),
        "gate": block_("L0_ffn_gate_w"),
        "w1": block_("L0_ffn_fc1_w"),
        "b1": np.ascontiguousarray(block_("L0_ffn_fc1_b").reshape(E, KT, P).transpose(0, 2, 1)),
        "w2": block_("L0_ffn_fc2_w"),
        "b2": block_("L0_ffn_fc2_b"),
        "alpha": rows(block_("L0_ffn_alpha"), P),
        "ident_f": np.eye(P, dtype=np.float32),
        "ident_b": np.eye(P).astype(bf),
        "mask_neg": np.where(low, 0.0, NEG).astype(bf),
        "mask_negT": np.where(low.T, 0.0, NEG).astype(bf),
        "k_rows": heads(k_rows),
        "q_rows": heads(q_rows),
        "e_index": rows(np.arange(E, dtype=np.float32), P),
    }
    nc = bacc.Bacc("TRN2", target_bir_lowering=False, num_devices=1)
    arrays, aps = {}, []
    for name, a in args.items():
        a = np.ascontiguousarray(a)
        arrays[f"in_{name}"] = a
        aps.append(nc.dram_tensor(f"in_{name}", a.shape, mybir.dt.from_np(a.dtype), kind="ExternalInput").ap())
    out = nc.dram_tensor("out", (B, T, D), fp32, kind="ExternalOutput").ap()
    attention_moe_kernel(nc, *aps, out)
    r = run_bass_kernel_spmd(nc, [arrays], core_ids=[0])
    return r.results[0]["out"]
```

```python
import concourse.bass as bass
from concourse import mybir
from contextlib import ExitStack

fp32 = mybir.dt.float32
bf16 = mybir.dt.bfloat16
i32 = mybir.dt.int32
ALU = mybir.AluOpType
ACT = mybir.ActivationFunctionType
AX = mybir.AxisListType

P = 128
B, T, D = 4, 1024, 256
H, HD = 16, 16
E = 8
KT = D // P
TB = T // P
NT = B * TB
HQ = 4
NQ = B * H // HQ
QF = HQ * HD
SCALE = HD ** -0.5
EPS = 1e-5
NEG = -3.0e38
BANK = 512

K_PART = (0, 0, 1, 1, 0, 2)
Q_PART = (0, 1, 0, 1, 2, 0)
NSPLIT = 3
DATA_ROWS = len(K_PART) * HD
DECAY_ROWS = (TB - 1) + 2
SCORE_ROWS = DATA_ROWS + DECAY_ROWS
ALL_ROWS = SCORE_ROWS + NSPLIT

PIECES = []
for ib in range(TB):
    for seg in range(0, P * (ib + 1), BANK):
        width = min(BANK, P * (ib + 1) - seg)
        heads = 4 if width == P else 2 if width == 2 * P else 1
        PIECES += [(ib, seg, width, h, heads) for h in range(0, HQ, heads)]
if len(PIECES) % 2 == 0:
    ib, seg, width, h, heads = PIECES.pop(1)
    PIECES[1:1] = [(ib, seg, width, h + n, 1) for n in range(heads)]
NP = len(PIECES)
PRO = NP + 1
WIN = PRO + 2
TYPES = [[[(0, h, 0)] for h in range(HQ)]]
for jb in range(1, TB // 2):
    TYPES.append([[(jb, h, 0), (TB - jb, h, T - P * jb)] for h in range(HQ)])
TYPES.append([[(TB // 2, h, 0), (TB // 2, h + 1, T // 2)] for h in range(0, HQ, 2)])
NTY = len(TYPES)
UNITS = [(k, n, parts) for k, units in enumerate(TYPES) for n, parts in enumerate(units)]
NU = len(UNITS)
LAST_OF_TYPE = [sum(len(u) for u in TYPES[:k + 1]) for k in range(NTY)]
SLOT = {(k, u): HQ * (k % 2) + ((u + 2) % HQ if k == 0 else u) for k, u, _ in UNITS}
NSLOT = 2 * HQ
GROUPS = [(k, jb, c) for k in range(NTY) for jb in sorted({p[0] for u in TYPES[k] for p in u})
          for c in range(2) if P * jb < (c + 1) * BANK]
LAG = 1
SPREAD = 13
AUG = 3
ROUNDS = 4
FIRST_TAIL = 1 + AUG * ROUNDS

SLOTS = (2 * B * T + E * (P - 1)) // P
SLOTS += -SLOTS % 4
CH = 4
SC = 16


NCONST = 16 + 2 * AUG


def rnd_of(n, j):
    return n // CH if isinstance(n, int) else LOOP_ROUND[0] + j // CH


LOOP_ROUND = [None]


def skewed(eng, stages):
    most = 3
    for n in range(-most, 0):
        for what, ahead in stages:
            if n + ahead >= 0:
                what(n + ahead, n + ahead)
    with eng.Fori(0, SLOTS // CH - 1) as t:
        LOOP_ROUND[0] = t
        for j in range(CH):
            for what, ahead in stages:
                what(CH * t + j + ahead, j + ahead)
    for n in range(SLOTS - CH, SLOTS):
        for what, ahead in stages:
            if n + ahead < SLOTS:
                what(n + ahead, n + ahead)


def attention_moe_kernel(nc, x, wqT, wkT, wvT, woT, qb, kb, vb, ob, gate, w1, b1, w2, b2, alpha,
                         ident_f, ident_b, mask_neg, mask_negT, before, k_rows, q_rows, numbers, out):
    x_t = x.rearrange("b (t p) d -> p (b t) d", p=P)
    out_t = out.rearrange("b (t p) d -> p (b t) d", p=P)

    ctx = ExitStack()
    with ctx:
        def sb(name, shape, dt=fp32):
            return ctx.enter_context(nc.sbuf_tensor(name, shape, dt))

        def sem(name):
            return ctx.enter_context(nc.semaphore(name))

        k_parts = nc.dram_tensor("k_parts", [NSPLIT, NQ * QF, T], bf16).ap()
        q_parts = nc.dram_tensor("q_parts", [NSPLIT, NQ * QF, T], bf16).ap()
        xn_dram = nc.dram_tensor("xn_dram", [B * T, D], fp32).ap()
        a_dram = nc.dram_tensor("a_dram", [NQ * TB * P, QF], fp32).ap()
        slot_dram = nc.dram_tensor("slot_dram", [P * SLOTS, 1], i32).ap()
        y_dram = nc.dram_tensor("y_dram", [SLOTS * P, D], fp32).ap()
        xn_t = xn_dram.rearrange("(t p) d -> p t d", p=P)
        a_q = a_dram.rearrange("(q t p) f -> p q t f", p=P, t=TB)
        a_t = a_dram.rearrange("(b g t p) f -> p b t g f", p=P, t=TB, g=HQ)

        wq_sb = sb("wq_sb", [P, KT, D])
        wk_sb = sb("wk_sb", [P, KT, D])
        wvg_sb = sb("wvg_sb", [P, KT, D + E])
        wo_sb = sb("wo_sb", [P, KT, D])
        qb_sb = sb("qb_sb", [P, KT])
        kb_sb = sb("kb_sb", [P, KT])
        kbs_sb = sb("kbs_sb", [P, KT])
        vb_sb = sb("vb_sb", [P, D])
        ob_sb = sb("ob_sb", [P, D])
        w1_sb = sb("w1_sb", [P, E * KT, D])
        w2_sb = sb("w2_sb", [P, E * KT, D])
        alpha_sb = sb("alpha_sb", [P, E])
        num_sb = sb("num_sb", [P, numbers.shape[1]])
        idf = sb("idf", [P, P])
        idb = sb("idb", [P, P], bf16)
        mask_sb = sb("mask_sb", [P, P], bf16)
        maskT_sb = sb("maskT_sb", [P, P], bf16)
        before_sb = sb("before_sb", [P, 2 * P], bf16)
        v_all = sb("v_all", [P, NQ, TB, QF])
        logits = sb("logits", [P, NT, E])
        weight = sb("weight", [P, NT, 2])
        slot = sb("slot", [P, NT, 2], i32)
        place = sb("place", [P, NT, 2], i32)
        tile_expert = sb("tile_expert", [P, SLOTS], i32)
        token_of = sb("token_of", [P, SLOTS], i32)
        token_id = sb("token_id", [P, NT, 2], i32)
        place_now = sb("place_now", [P, SC], i32)
        token_now = sb("token_now", [P, SC], i32)
        rows_now = sb("rows_now", [P, 2, CH], i32)
        picked_b = sb("picked_b", [P, NT, E], bf16)
        ARENA = 16 * 1024
        arena = sb("arena", [P, ARENA])
        at = [0]

        def cut(cols, dt=fp32):
            words = cols if dt == fp32 else cols // 2
            a = arena[:, at[0]:at[0] + words]
            at[0] += words
            assert at[0] <= ARENA
            return a if dt == fp32 else a.bitcast(dt)

        xb = cut(TB * D).rearrange("p (t d) -> p t d", d=D)
        xnb = cut(TB * D).rearrange("p (t d) -> p t d", d=D)
        xnT = cut(KT * T).rearrange("p (k t) -> p k t", k=KT)
        whole = [cut(T) for _ in range(4)]
        parts = [cut(NSPLIT * T, bf16).rearrange("p (s t) -> p s t", s=NSPLIT) for _ in range(4)]
        at[0] = 0
        gat = [cut(NT * E).rearrange("p (t e) -> p t e", e=E) for _ in range(7)]
        col = [cut(NT) for _ in range(8)]
        need = cut(E * NT).rearrange("p (e k) -> p e k", e=E)
        ahead = cut(E * E).rearrange("p (e f) -> p e f", e=E)
        full = cut(SLOTS * (E - 1)).rearrange("p (n e) -> p n e", e=E - 1)
        some = [cut(E) for _ in range(4)]
        expert_f = cut(SLOTS)
        slot_f = cut(NT * 2).rearrange("p (t k) -> p t k", k=2)
        hi_i = cut(NT * 2).bitcast(i32).rearrange("p (t k) -> p t k", k=2)
        lo_i = cut(NT * 2).bitcast(i32).rearrange("p (t k) -> p t k", k=2)
        at[0] = 0
        probs = [cut(T) for _ in range(NSLOT)]
        oT = cut(T)
        a_out_sb = [cut(TB * QF).rearrange("p (t f) -> p t f", f=QF) for _ in range(AUG)]
        at[0] = ARENA - 2 * E * D
        b1_sb = cut(E * D).rearrange("p (e n) -> p e n", e=E)
        b2_sb = cut(E * D).rearrange("p (e n) -> p e n", e=E)
        at[0] = 0
        xg = [cut(D) for _ in range(CH)]
        xgT = [cut(D) for _ in range(2)]
        hid = [cut(D) for _ in range(2)]
        hidT = [cut(D) for _ in range(2)]
        ysb = [cut(D) for _ in range(CH)]
        xo = [cut(2 * D) for _ in range(2)]
        a_tok = [cut(2 * D) for _ in range(2)]
        aT = [cut(2 * D) for _ in range(2)]
        ya = [[cut(D) for _ in range(4)] for _ in range(2)]
        gsum = [cut(2 * D) for _ in range(2)]
        so = [cut(2 * D) for _ in range(2)]
        assert at[0] <= ARENA - 2 * E * D

        k_aug = [sb(f"k_aug{n}", [P, HQ, T], bf16) for n in range(AUG)]
        q_aug = [sb(f"q_aug{n}", [P, HQ, T], bf16) for n in range(AUG)]
        v_q = [sb(f"v_q{n}", [P, TB, HQ, 2 * HD]) for n in range(AUG)]
        mxa = sb("mxa", [P, HQ, TB])
        mxb = sb("mxb", [P, HQ, TB // 2])
        mrest = sb("mrest", [P, HQ, TB])
        msplit = sb("msplit", [P, NSPLIT * TB * HQ], bf16)
        mT = sb("mT", [NSPLIT * TB * HQ, P], bf16)
        rden = [sb(f"rden{n}", [P, TB // 2, HQ]) for n in range(2)]
        stats = sb("stats", [P, TB, 6])
        mv = sb("mv", [P, TB, 2])
        veps = sb("veps", [P, TB])
        std = sb("std", [P, TB])
        rstd = sb("rstd", [P, TB])

        ps = ctx.enter_context(nc.psum_tensor("ps", [P, 8 * BANK], fp32))

        def bank(n, k=1):
            return ps[:, n * BANK:(n + k) * BANK]

        consts_in = sem("consts_in"); bias_ready = sem("bias_ready")
        x_in = sem("x_in"); xb_free = sem("xb_free")
        var_ready = sem("var_ready"); std_ready = sem("std_ready"); xn_ready = sem("xn_ready")
        xn_out = sem("xn_out")
        xpose_done = sem("xpose_done"); xT_ready = sem("xT_ready")
        proj_done = sem("proj_done"); proj_out = sem("proj_out"); split_done = sem("split_done")
        parts_out = sem("parts_out")
        v_done = sem("v_done"); v_out = sem("v_out")
        ln_step = sem("ln_step"); split_step = sem("split_step"); gate_step = sem("gate_step")
        m_step = sem("m_step"); o_step = sem("o_step"); fin_step = sem("fin_step")
        passed = sem("passed")
        gap_ready = sem("gap_ready"); gexp_ready = sem("gexp_ready")
        picked = sem("picked"); counted = sem("counted"); routed = sem("routed")
        zeros_set = sem("zeros_set"); slots_zero = sem("slots_zero")
        scat_ready = sem("scat_ready"); scattered = sem("scattered"); slots_in = sem("slots_in")
        moe_w_in = sem("moe_w_in")
        ones_set = sem("ones_set"); vq_ready = sem("vq_ready")
        aug_in = [sem(f"aug_in{n}") for n in range(AUG)]
        piece_done = sem("piece_done"); piece_used = sem("piece_used")
        m_split = sem("m_split"); mT_ready = sem("mT_ready"); m_in = sem("m_in")
        s_done = sem("s_done"); exp_done = sem("exp_done")
        pv_done = sem("pv_done"); o_out = sem("o_out")
        a_ready = sem("a_ready"); a_stored = [sem(f"a_stored{n}") for n in range(AUG)]
        rows_ready = sem("rows_ready"); xg_in = [sem(f"xg_in{n}") for n in range(CH)]
        t1_done = sem("t1_done"); xgT_out = sem("xgT_out"); l1_done = sem("l1_done"); h_out = sem("h_out")
        g_done = sem("g_done"); t2_done = sem("t2_done"); gT_out = sem("gT_out"); l2_done = sem("l2_done")
        y_out = sem("y_out"); y_stored = [sem(f"y_stored{n}") for n in range(CH)]
        xo_in = [sem(f"xo_in{n}") for n in range(2)]; a_in = [sem(f"a_in{n}") for n in range(2)]
        ya_in = [sem(f"ya_in{n}") for n in range(2)]
        at_done = sem("at_done"); at_out = sem("at_out"); sg_done = sem("sg_done"); sg_used = sem("sg_used")
        ya_used = sem("ya_used")
        gsum_done = sem("gsum_done"); silu_done = sem("silu_done"); fin_done = sem("fin_done")
        stored = [sem(f"stored{n}") for n in range(2)]

        SIDES = [(side, m) for side in range(2) for m in range(KT)]
        PROJ = [(n, c) for n in range(4) for c in range(T // BANK)]

        e_index = num_sb[:, 0:E]
        at_num = E
        multiples = num_sb[:, at_num:at_num + NT]
        at_num += NT
        is_ahead = num_sb[:, at_num:at_num + E * E].rearrange("p (e f) -> p e f", e=E)
        at_num += E * E
        tile_index = num_sb[:, at_num:at_num + SLOTS]
        at_num += SLOTS
        token_f = num_sb[:, at_num:at_num + NT]
        assert at_num + NT == numbers.shape[1]

        block = ctx.enter_context(nc.Block())

        @block.sync
        def _(sp):
            sp.sem_inc(parts_out, 16 * 4)
            for n in range(AUG):
                sp.sem_inc(a_stored[n], 16)
            for n in range(CH):
                sp.sem_inc(y_stored[n], 16)
            for par in range(2):
                sp.sem_inc(stored[par], 16)
            sp.dma_start(xb, x_t[:, 0:TB, :]).then_inc(x_in, 16)
            weights = lambda w: w.rearrange("(k p) n -> p k n", p=P)
            loads = [(idf[:, :], ident_f), (wk_sb[:, :, :], weights(wkT)), (wq_sb[:, :, :], weights(wqT)),
                     (qb_sb[:, :], qb), (kb_sb[:, :], kb), (vb_sb[:, :], vb),
                     (wvg_sb[:, :, 0:D], weights(wvT)), (wvg_sb[:, :, D:D + E], weights(gate)),
                     (wo_sb[:, :, :], weights(woT)), (ob_sb[:, :], ob), (alpha_sb[:, :], alpha),
                     (num_sb[:, :], numbers), (idb[:, :], ident_b), (mask_sb[:, :], mask_neg),
                     (maskT_sb[:, :], mask_negT), (before_sb[:, :], before)]
            for n in range(AUG):
                loads += [(k_aug[n][DATA_ROWS:SCORE_ROWS], k_rows), (q_aug[n][DATA_ROWS:ALL_ROWS], q_rows)]
            assert len(loads) == NCONST
            for dst, src in loads:
                sp.dma_start(dst, src).then_inc(consts_in, 16)

            def batch(b, last):
                if not last:
                    sp.wait_ge(xb_free, b + 1)
                    sp.dma_start(xb, x_t[:, bass.ds(TB * b + TB, TB), :]).then_inc(x_in, 16)
                sp.wait_ge(xn_ready, b + 1)
                sp.dma_start(xn_t[:, bass.ts(b, TB), :], xnb).then_inc(xn_out, 16)
                for n, (side, m) in enumerate(SIDES):
                    sp.wait_ge(split_done, 4 * b + n + 5)
                    dst = (k_parts, q_parts)[side]
                    sp.dma_start(dst[:, bass.ds(b * D + m * P, P), :].rearrange("s p t -> p s t"),
                                 parts[n]).then_inc(parts_out, 16)

            def load_quad(q, n):
                for g in range(len(K_PART)):
                    rows = slice(HD * g, HD * (g + 1))
                    for aug, src, part in ((k_aug, k_parts, K_PART[g]), (q_aug, q_parts, Q_PART[g])):
                        sp.dma_start(aug[n][rows, :, :],
                                     src[part, bass.ts(q, QF), :].rearrange("(h d) t -> d h t", d=HD)
                                     ).then_inc(aug_in[n], 16)

            def load_maxima(q, n):
                sp.wait_ge(mT_ready, q + 1)
                for s in range(NSPLIT):
                    dst = k_aug[n][SCORE_ROWS + s:SCORE_ROWS + s + 1, :, :]
                    rows = mT[s * TB * HQ:(s + 1) * TB * HQ, :]
                    sp.dma_start(dst.rearrange("o h (t i) -> o (h t) i", t=TB), rows).then_inc(m_in, 16)

            def store_quad(q, n):
                sp.wait_ge(a_ready, q + 1)
                sp.dma_start(a_q[:, q, :, :], a_out_sb[n]).then_inc(a_stored[n], 16)

            with sp.Fori(0, B - 1) as b:
                batch(b, False)
            sp.wait_ge(parts_out, 64 * B)
            load_quad(0, 0)
            load_quad(1, 1)
            batch(B - 1, True)
            load_maxima(0, 0)
            sp.wait_ge(zeros_set, 1)
            sp.dma_start(slot_dram.rearrange("(p n) o -> p (n o)", p=P), token_of[:, :]).then_inc(slots_zero, 16)
            sp.wait_ge(parts_out, 64 * (B + 1))

            def window(q, n):
                if not isinstance(q, int) or q + 2 < NQ:
                    sp.wait_ge(s_done, NU * q + 1)
                    load_quad(q + 2, (n + 2) % AUG)
                if not isinstance(q, int) or q > 0:
                    store_quad(q - 1, (n + 2) % AUG)
                if not isinstance(q, int) or q + 1 < NQ:
                    load_maxima(q + 1, (n + 1) % AUG)

            window(0, 0)
            for dst, src in ((w1_sb, w1.rearrange("e (k p) n -> p (e k) n", p=P)),
                             (w2_sb, w2.rearrange("e (k p) n -> p (e k) n", p=P)), (b1_sb, b1), (b2_sb, b2)):
                sp.dma_start(dst[:, :, :], src).then_inc(moe_w_in, 16)
            with sp.Fori(0, ROUNDS) as t:
                for r in range(AUG):
                    window(AUG * t + r + 1, (r + 1) % AUG)
            for q in range(FIRST_TAIL, NQ):
                window(q, q % AUG)
            store_quad(NQ - 1, (NQ - 1) % AUG)

            with sp.Fori(0, SLOTS // CH) as t:
                for j in range(CH):
                    n = CH * t + j
                    sp.wait_ge(y_out, n + 3)
                    sp.dma_start(y_dram[bass.ts(n, P), :], ysb[j]).then_inc(y_stored[j], 16)

            for n in range(AUG):
                sp.wait_ge(a_stored[n], 16 * ((NQ - 1 - n) // AUG + 2))
            with sp.Fori(0, NT // 4) as t:
                for par in range(2):
                    n = 2 * t + par
                    sp.wait_ge(stored[par], 16 * t + 16)
                    sp.dma_start(xo[par].rearrange("p (t d) -> p t d", d=D),
                                 x_t[:, bass.ts(n, 2), :]).then_inc(xo_in[par], 16)
                    sp.wait_ge(at_done, n + 1)
                    for j in range(2):
                        sp.dma_start(a_tok[par][:, j * D:(j + 1) * D].rearrange("p (g f) -> p g f", f=QF),
                                     a_t[:, n // (TB // 2), 2 * (n % (TB // 2)) + j, :, :]).then_inc(a_in[par], 16)
                for par in range(2):
                    n = 2 * t + par
                    sp.wait_ge(fin_done, n + 1)
                    sp.dma_start(out_t[:, bass.ts(n, 2), :],
                                 xo[par].rearrange("p (t d) -> p t d", d=D)).then_inc(stored[par], 16)
            for par in range(2):
                sp.wait_ge(stored[par], 16 * (NT // 4) + 16)

        @block.gpsimd
        def _(pool):
            nc.gpsimd.memset(token_of[:, :], 0).then_inc(zeros_set, 1)
            for n in range(AUG):
                nc.gpsimd.memset(v_q[n][:, :, :, HD:2 * HD], 1.0).then_inc(ones_set, 1)

            def take_v(q, n):
                nc.gpsimd.tensor_copy(v_q[n][:, :, :, 0:HD],
                                      v_all[:, q, :, :].rearrange("p t (h d) -> p t h d", d=HD)
                                      ).then_inc(vq_ready, 1)

            def next_v(q, n):
                pool.wait_ge(pv_done, NTY * q + 2)
                take_v(q + 1, (n + 1) % AUG)

            pool.wait_ge(v_out, NT + 2)
            take_v(0, 0)
            next_v(0, 0)
            pool.wait_ge(routed, 1)
            nc.gpsimd.tensor_copy(token_id[:, :, 0], token_f)
            nc.gpsimd.tensor_copy(token_id[:, :, 1], token_f).then_inc(scat_ready, 1)
            pool.wait_ge(scat_ready, 1)
            pool.wait_ge(slots_zero, 16)
            with pool.Fori(0, ROUNDS) as t:
                for r in range(AUG):
                    next_v(AUG * t + r + 1, (r + 1) % AUG)
                    rounds = NT * 2 // SC // ROUNDS
                    if r < rounds:
                        i = rounds * t + r
                        nc.gpsimd.tensor_copy(place_now[:, :], place[:, bass.ts(i, SC // 2), :])
                        nc.gpsimd.tensor_copy(token_now[:, :], token_id[:, bass.ts(i, SC // 2), :]).then_inc(scat_ready, 1)
                        pool.wait_ge(scat_ready, i + 2)
                        pool.sem_inc(passed, 1)
                        for s in range(SC):
                            nc.gpsimd.indirect_dma_start(
                                out=slot_dram, out_offset=bass.IndirectOffsetOnAxis(ap=place_now[:, s:s + 1], axis=0),
                                in_=token_now[:, s:s + 1], in_offset=None).then_inc(scattered, 16)
                        pool.wait_ge(scattered, 16 * SC * i + 16 * SC)
                        pool.sem_inc(passed, 1)
            for q in range(FIRST_TAIL, NQ - 1):
                next_v(q, q % AUG)
            pool.wait_ge(scattered, 16 * 2 * NT)
            pool.dma_start(token_of[:, :], slot_dram.rearrange("(p n) o -> p (n o)", p=P)).then_inc(slots_in, 16)
            pool.wait_ge(slots_in, 16)
            pool.wait_ge(xn_out, 16 * B)
            pool.wait_ge(pv_done, NTY * NQ + 2)
            with pool.Fori(0, SLOTS // CH) as t:
                pool.wait_ge(t1_done, CH * t + CH)
                nc.gpsimd.tensor_copy(rows_now[:, 0, :], token_of[:, bass.ts(t, CH)]).then_inc(rows_ready, 1)
                pool.wait_ge(rows_ready, t + 1)
                pool.sem_inc(passed, 1)
                for j in range(CH):
                    nc.gpsimd.indirect_dma_start(
                        out=xg[j], out_offset=None, in_=xn_dram,
                        in_offset=bass.IndirectOffsetOnAxis(ap=rows_now[:, 0, j:j + 1], axis=0)).then_inc(xg_in[j], 16)
            for j in range(CH):
                pool.wait_ge(xg_in[j], 16 * (SLOTS // CH))
                pool.wait_ge(y_stored[j], 16 * (SLOTS // CH) + 16)
            with pool.Fori(0, NT // 4) as t:
                for par in range(2):
                    n = 2 * t + par
                    pool.wait_ge(ya_used, n + 1)
                    nc.gpsimd.tensor_copy(rows_now[:, par, :], slot[:, bass.ts(n, 2), :]).then_inc(rows_ready, 1)
                    pool.wait_ge(rows_ready, SLOTS // CH + n + 1)
                    pool.sem_inc(passed, 1)
                    for j in range(4):
                        nc.gpsimd.indirect_dma_start(
                            out=ya[par][j], out_offset=None, in_=y_dram,
                            in_offset=bass.IndirectOffsetOnAxis(ap=rows_now[:, par, j:j + 1], axis=0)
                        ).then_inc(ya_in[par], 16)

        @block.scalar
        def _(act):
            act.sem_inc(xT_ready, 4)
            act.sem_inc(proj_out, 2)
            act.sem_inc(exp_done, 2)
            act.sem_inc(o_out, 1)
            act.sem_inc(xgT_out, 2)
            act.sem_inc(gT_out, 2)
            act.sem_inc(at_out, 2)
            act.sem_inc(silu_done, 2)

            def roots(b):
                act.wait_ge(var_ready, b + 1)
                nc.scalar.activation(std[:, :], veps[:, :], ACT.Sqrt).then_inc(std_ready, 1)

            act.wait_ge(consts_in, 16 * NCONST)
            act.wait_ge(bias_ready, 1)
            roots(0)

            def batch(b, last):
                act.wait_ge(v_out, TB * b + 2)
                for n in range(4):
                    act.wait_ge(xpose_done, 4 * b + n + 5)
                    half, k = divmod(n, 2)
                    nc.scalar.activation(xnT[:, k, half * BANK:(half + 1) * BANK], bank(n),
                                         ACT.Copy).then_inc(xT_ready, 1)
                act.wait_ge(parts_out, 64 * b + 64)
                for i, (n, c) in enumerate(PROJ):
                    side, m = SIDES[n]
                    act.wait_ge(proj_done, 8 * b + i + 1)
                    if c == 0:
                        act.wait_ge(split_done, 4 * b + n + 1)
                    cs = slice(c * BANK, (c + 1) * BANK)
                    bias = (kbs_sb, qb_sb)[side][:, m:m + 1]
                    scale = (SCALE, 1.0)[side]
                    nc.scalar.activation(whole[n][:, cs], bank(4 + i % 2), ACT.Identity, bias=bias, scale=scale)
                    nc.scalar.activation(parts[n][:, 0, cs], bank(4 + i % 2), ACT.Identity, bias=bias,
                                         scale=scale).then_inc(proj_out, 1)
                if not last:
                    roots(b + 1)

            with act.Fori(0, B - 1) as b:
                batch(b, False)
            batch(B - 1, True)
            act.wait_ge(gap_ready, 1)
            nc.scalar.activation(col[4], col[3], ACT.Exp).then_inc(gexp_ready, 1)
            act.wait_ge(routed, 1)

            def window(q):
                for n, (k, u, unit) in enumerate(UNITS):
                    if k == 0 and u == 0:
                        act.wait_ge(pv_done, NTY * q + 1)
                    elif k > 0 and u == 0 or k == 0 and SLOT[k, u] == 0:
                        act.wait_ge(pv_done, NTY * q + max(k - 1, 0) + 2)
                    act.wait_ge(s_done, NU * q + n + 2)
                    nc.scalar.activation(probs[SLOT[k, u]], bank(2 + 2 * (n % 2), 2), ACT.Exp).then_inc(exp_done, 1)
                act.wait_ge(pv_done, NTY * q + NTY + 2)
                nc.scalar.activation(oT, bank(6, 2), ACT.Copy).then_inc(o_out, 1)

            window(0)
            with act.Fori(0, ROUNDS) as t:
                for r in range(AUG):
                    window(AUG * t + r + 1)
            for q in range(FIRST_TAIL, NQ):
                window(q)

            def x_evacuate(n, j):
                act.wait_ge(t1_done, n + 1 + CH)
                nc.scalar.activation(xgT[j % 2], bank(j % 2)[:, 0:D], ACT.Copy).then_inc(xgT_out, 1)

            def gelu(n, j):
                act.wait_ge(h_out, n + 3)
                nc.scalar.activation(hid[j % 2], hid[j % 2], ACT.Gelu).then_inc(g_done, 1)

            def g_evacuate(n, j):
                act.wait_ge(t2_done, n + 1)
                nc.scalar.activation(hidT[j % 2], bank(4 + j % 2)[:, 0:D], ACT.Copy).then_inc(gT_out, 1)

            act.wait_ge(piece_used, PRO + WIN * (NQ - 1) + 4)
            skewed(act, ((x_evacuate, 3), (gelu, 2), (g_evacuate, 1)))

            with act.Fori(0, NT // 4) as t:
                for par in range(2):
                    n = 2 * t + par
                    act.wait_ge(at_done, n + 3)
                    nc.scalar.activation(aT[par], bank(4 * par), ACT.Copy).then_inc(at_out, 1)
                    act.wait_ge(gsum_done, n + 1)
                    nc.scalar.activation(gsum[par], gsum[par], ACT.Silu).then_inc(silu_done, 1)

        @block.vector
        def _(dve):
            def spread(ap, n):
                return bass.AP(ap.tensor, ap.offset, [list(x) for x in ap.ap] + [[0, n]])

            def over(ap, n):
                return bass.AP(ap.tensor, ap.offset, [list(ap.ap[0]), [0, n]] + [list(x) for x in ap.ap[1:]])

            dve.sem_inc(split_done, 4)
            dve.sem_inc(v_out, 2)
            dve.sem_inc(piece_used, 2)
            dve.sem_inc(h_out, 2)
            dve.sem_inc(y_out, 2)
            dve.sem_inc(ya_used, 2)
            dve.sem_inc(sg_used, 2)

            def normalise(b):
                dve.wait_ge(x_in, 16 * b + 16)
                for t in range(TB):
                    ins = nc.vector.bn_stats(stats[:, t, :], xb[:, t, :])
                ins.then_inc(ln_step, 1)
                dve.wait_ge(ln_step, 3 * b + 1)
                dve.sem_inc(passed, 1)
                for t in range(TB):
                    ins = nc.vector.bn_aggr(mv[:, t, :], stats[:, t, :])
                ins.then_inc(ln_step, 1)
                dve.wait_ge(ln_step, 3 * b + 2)
                nc.vector.tensor_scalar(veps[:, :], mv[:, :, 1], EPS, None, ALU.add).then_inc(var_ready, 1)
                dve.wait_ge(std_ready, b + 1)
                nc.vector.reciprocal(rstd[:, :], std[:, :]).then_inc(ln_step, 1)
                dve.wait_ge(ln_step, 3 * b + 3)
                dve.wait_ge(xpose_done, 4 * b + 4)
                if not isinstance(b, int) or b > 0:
                    dve.wait_ge(xn_out, 16 * b)
                for t in range(TB):
                    ins = nc.vector.tensor_scalar(xnb[:, t, :], xb[:, t, :], mv[:, t, 0:1], rstd[:, t:t + 1],
                                                  ALU.subtract, ALU.mult)
                ins.then_inc(xn_ready, 1)
                dve.wait_ge(xn_ready, b + 1)
                dve.sem_inc(xb_free, 1)

            def batch(b, last):
                for n in range(4):
                    dve.wait_ge(proj_out, 8 * b + 2 * n + 4)
                    nc.vector.tensor_tensor(whole[n], whole[n], parts[n][:, 0, :],
                                            ALU.subtract).then_inc(split_step, 1)
                    dve.wait_ge(split_step, 8 * b + 2 * n + 1)
                    nc.vector.tensor_copy(parts[n][:, 1, :], whole[n]).then_inc(split_step, 1)
                    dve.wait_ge(split_step, 8 * b + 2 * n + 2)
                    nc.vector.tensor_tensor(parts[n][:, 2, :], whole[n], parts[n][:, 1, :],
                                            ALU.subtract).then_inc(split_done, 1)
                    if n == 0 and not last:
                        normalise(b + 1)
                for t in range(TB):
                    dve.wait_ge(v_done, TB * b + t + 1)
                    vp = bank(6 + t % 2)
                    nc.vector.tensor_tensor(v_all[:, bass.ts(b, HQ), t, :],
                                            vp[:, 0:D].rearrange("p (g f) -> p g f", f=QF),
                                            vb_sb[:, :].rearrange("p (g f) -> p g f", f=QF), ALU.add)
                    nc.vector.tensor_copy(logits[:, TB * b + t, :], vp[:, D:D + E]).then_inc(v_out, 1)

            dve.wait_ge(consts_in, 16 * NCONST)
            nc.vector.tensor_scalar(kbs_sb[:, :], kb_sb[:, :], SCALE, None, ALU.mult).then_inc(bias_ready, 1)
            normalise(0)
            with dve.Fori(0, B - 1) as b:
                batch(b, False)
            batch(B - 1, True)

            step = [0]

            def after(ins):
                step[0] += 1
                ins.then_inc(gate_step, 1)
                dve.wait_ge(gate_step, step[0])

            dve.wait_ge(v_out, NT + 2)
            dve.wait_ge(xn_out, 16 * B)
            index = over(e_index, NT)
            best, first, second, gap, gexp, where, norm, low = col

            def choose(values, top, chosen):
                after(nc.vector.tensor_reduce(top, values, AX.X, ALU.max))
                after(nc.vector.tensor_tensor(gat[0], values, spread(top, E), ALU.is_lt))
                after(nc.vector.scalar_tensor_tensor(gat[0], gat[0], float(E), index, ALU.mult, ALU.add))
                after(nc.vector.tensor_reduce(where, gat[0], AX.X, ALU.min))
                after(nc.vector.tensor_tensor(chosen, index, spread(where, E), ALU.is_equal))

            choose(logits[:, :, :], best, gat[1])
            after(nc.vector.scalar_tensor_tensor(gat[2], gat[1], NEG, logits[:, :, :], ALU.mult, ALU.add))
            choose(gat[2], second, gat[3])
            nc.vector.tensor_tensor(gap, second, best, ALU.subtract).then_inc(gap_ready, 1)
            after(nc.vector.tensor_tensor(picked_b[:, :, :], gat[1], gat[3], ALU.add))
            dve.sem_inc(picked, 1)
            dve.wait_ge(gexp_ready, 1)
            after(nc.vector.tensor_scalar(norm, gexp, 1.0, None, ALU.add))
            after(nc.vector.reciprocal(first, norm))
            after(nc.vector.tensor_tensor(low, gexp, first, ALU.mult))
            for k, share in ((0, first), (1, low)):
                after(nc.vector.tensor_tensor(gat[0], gat[1 + 2 * k], over(alpha_sb[:, :], NT), ALU.mult))
                after(nc.vector.tensor_reduce(where, gat[0], AX.X, ALU.add))
                after(nc.vector.tensor_tensor(weight[:, :, k], where, share, ALU.mult))
            dve.wait_ge(counted, 1)
            ahead_ps = bank(6)[:, 0:NT * E].rearrange("p (t e) -> p t e", e=E)
            of_tile = bank(7)[:, 0:NT * E].rearrange("p (t e) -> p t e", e=E)
            after(nc.vector.tensor_copy(gat[4], of_tile))
            src, dst, by = gat[4], gat[5], 1
            while by < NT:
                nc.vector.tensor_copy(dst[:, 0:by, :], src[:, 0:by, :])
                after(nc.vector.tensor_tensor(dst[:, by:, :], src[:, by:, :], src[:, 0:NT - by, :], ALU.add))
                src, dst, by = dst, src, 2 * by
            tiles, base, upto, _ = some
            after(nc.vector.tensor_tensor(need, spread(src[:, NT - 1, :], NT), over(multiples, E), ALU.is_gt))
            after(nc.vector.tensor_reduce(tiles, need, AX.X, ALU.add))
            after(nc.vector.tensor_tensor(ahead, over(tiles, E), is_ahead, ALU.mult))
            after(nc.vector.tensor_reduce(base, ahead, AX.X, ALU.add))
            after(nc.vector.tensor_tensor(upto, base, tiles, ALU.add))
            after(nc.vector.tensor_tensor(dst, src, of_tile, ALU.subtract))
            after(nc.vector.tensor_tensor(dst, dst, ahead_ps, ALU.add))
            after(nc.vector.scalar_tensor_tensor(dst, over(base, NT), float(P), dst, ALU.mult, ALU.add))
            for k in range(2):
                after(nc.vector.tensor_tensor(gat[0], gat[1 + 2 * k], dst, ALU.mult))
                after(nc.vector.tensor_reduce(slot_f[:, :, k], gat[0], AX.X, ALU.add))
            after(nc.vector.tensor_copy(slot[:, :, :], slot_f))
            after(nc.vector.tensor_single_scalar(hi_i, slot[:, :, :], P.bit_length() - 1, ALU.arith_shift_right))
            after(nc.vector.tensor_single_scalar(lo_i, slot[:, :, :], P - 1, ALU.bitwise_and))
            after(nc.vector.scalar_tensor_tensor(place[:, :, :], lo_i, float(SLOTS), hi_i, ALU.mult, ALU.add))
            after(nc.vector.tensor_tensor(full, spread(tile_index, E - 1), over(upto[:, 0:E - 1], SLOTS), ALU.is_ge))
            after(nc.vector.tensor_reduce(expert_f, full, AX.X, ALU.add))
            after(nc.vector.tensor_copy(tile_expert[:, :], expert_f))
            dve.sem_inc(routed, 1)

            def reduce_piece(i, piece):
                ib, seg, width, h, heads = piece
                src = bank(i % 2)[:, 0:width * heads].rearrange("p (h j) -> p h j", h=heads)
                dst = mxb[:, h:h + heads, ib - TB // 2] if seg else mxa[:, h:h + heads, ib]
                return nc.vector.tensor_reduce(dst, src, AX.X, ALU.max)

            def maxima(q, base):
                for i, piece in enumerate(PIECES):
                    dve.wait_ge(piece_done, base + i + 1)
                    reduce_piece(i, piece).then_inc(piece_used, 1)
                dve.wait_ge(piece_used, base + NP + 2)
                dst = [msplit[:, s * TB * HQ:(s + 1) * TB * HQ].rearrange("p (h t) -> p h t", t=TB)
                       for s in range(NSPLIT)]
                nc.vector.tensor_tensor(mxa[:, :, TB // 2:TB], mxa[:, :, TB // 2:TB], mxb[:, :, :],
                                        ALU.max).then_inc(m_step, 1)
                dve.wait_ge(m_step, 4 * q + 1)
                nc.vector.tensor_copy(dst[0], mxa[:, :, :]).then_inc(m_step, 1)
                dve.wait_ge(m_step, 4 * q + 2)
                nc.vector.tensor_tensor(mrest[:, :, :], mxa[:, :, :], dst[0], ALU.subtract).then_inc(m_step, 1)
                dve.wait_ge(m_step, 4 * q + 3)
                nc.vector.tensor_copy(dst[1], mrest[:, :, :]).then_inc(m_step, 1)
                dve.wait_ge(m_step, 4 * q + 4)
                nc.vector.tensor_tensor(dst[2], mrest[:, :, :], dst[1], ALU.subtract).then_inc(m_split, 1)
                dve.wait_ge(piece_done, base + NP + 1)
                if not isinstance(q, int) or q > 0:
                    dve.wait_ge(m_in, 48 * q)
                nc.vector.tensor_copy(mT[:, :], bank(NP % 2).bitcast(bf16)[0:NSPLIT * TB * HQ, 0:P]
                                      ).then_inc(mT_ready, 1)
                dve.wait_ge(mT_ready, q + 1)
                dve.sem_inc(piece_used, 1)

            def outputs(q, n, rnd, base):
                dve.wait_ge(a_stored[n], 16 * rnd + 16)
                for half in range(2):
                    dve.wait_ge(piece_done, base + half + 1)
                    o = bank(half).rearrange("p (t h c) -> p t h c", t=TB // 2, h=HQ)
                    nc.vector.reciprocal(rden[half][:, :, :], o[:, :, :, HD]).then_inc(o_step, 1)
                    dve.wait_ge(o_step, 2 * q + half + 1)
                    dst = a_out_sb[n][:, half * TB // 2:(half + 1) * TB // 2, :]
                    ins = nc.vector.tensor_tensor(dst.rearrange("p t (h d) -> p t h d", d=HD), o[:, :, :, 0:HD],
                                                  spread(rden[half][:, :, :], HD), ALU.mult).then_inc(piece_used, 1)
                dve.wait_ge(piece_used, base + 4)
                dve.sem_inc(a_ready, 1)

            maxima(0, 0)
            maxima(1, PRO)
            with dve.Fori(0, ROUNDS) as t:
                for r in range(AUG):
                    q = AUG * t + r + 1
                    outputs(q - 1, r, t, PRO + WIN * q - 2)
                    maxima(q + 1, PRO + WIN * q)
            for q in range(FIRST_TAIL, NQ):
                outputs(q - 1, (q - 1) % AUG, (q - 1) // AUG, PRO + WIN * q - 2)
                if q + 1 < NQ:
                    maxima(q + 1, PRO + WIN * q)
            outputs(NQ - 1, (NQ - 1) % AUG, (NQ - 1) // AUG, PRO + WIN * (NQ - 1))

            def h_evacuate(n, j):
                dve.wait_ge(l1_done, n + 1)
                dve.sem_inc(passed, 1)
                e = dve.value_load(tile_expert[0:1, bass.ds(n, 1)], min_val=0, max_val=E - 1)
                nc.vector.tensor_tensor(hid[j % 2], bank(2 + j % 2)[:, 0:D], b1_sb[:, e, :], ALU.add).then_inc(h_out, 1)

            def y_evacuate(n, j):
                dve.wait_ge(l2_done, n + 1)
                dve.wait_ge(y_stored[j % CH], 16 * rnd_of(n, j) + 16)
                dve.sem_inc(passed, 1)
                e = dve.value_load(tile_expert[0:1, bass.ds(n, 1)], min_val=0, max_val=E - 1)
                nc.vector.tensor_tensor(ysb[j % CH], bank(6 + j % 2)[:, 0:D], b2_sb[:, e, :], ALU.add).then_inc(y_out, 1)

            dve.wait_ge(pv_done, NTY * NQ + 2)
            dve.wait_ge(moe_w_in, 64)
            skewed(dve, ((h_evacuate, 2), (y_evacuate, 0)))

            ob2 = over(ob_sb[:, :], 2)
            with dve.Fori(0, NT // 4) as t:
                for par in range(2):
                    n = 2 * t + par
                    dve.wait_ge(ya_in[par], 64 * t + 64)
                    dve.wait_ge(silu_done, n + 1)
                    for j in range(2):
                        ins = nc.vector.tensor_scalar(gsum[par][:, j * D:(j + 1) * D], ya[par][2 * j],
                                                      weight[:, 2 * n + j, 0:1], None, ALU.mult)
                    ins.then_inc(fin_step, 1)
                    dve.wait_ge(fin_step, 2 * n + 1)
                    for j in range(2):
                        ins = nc.vector.scalar_tensor_tensor(gsum[par][:, j * D:(j + 1) * D], ya[par][2 * j + 1],
                                                             weight[:, 2 * n + j, 1:2],
                                                             gsum[par][:, j * D:(j + 1) * D], ALU.mult, ALU.add)
                    ins.then_inc(gsum_done, 1)
                    dve.wait_ge(gsum_done, n + 1)
                    dve.sem_inc(ya_used, 1)
                    dve.wait_ge(sg_done, n + 1)
                    nc.vector.tensor_tensor(so[par].rearrange("p (t d) -> p t d", d=D),
                                            bank(4 * par + 2).rearrange("p (t d) -> p t d", d=D), ob2,
                                            ALU.add).then_inc(sg_used, 1)
                    dve.wait_ge(sg_used, n + 3)
                    dve.wait_ge(silu_done, n + 3)
                    nc.vector.tensor_tensor(so[par], so[par], gsum[par], ALU.mult).then_inc(fin_step, 1)
                    dve.wait_ge(fin_step, 2 * n + 2)
                    dve.wait_ge(xo_in[par], 16 * t + 16)
                    nc.vector.tensor_tensor(xo[par], xo[par], so[par], ALU.add).then_inc(fin_done, 1)

        @block.tensor
        def _(pe):
            pe.sem_inc(xpose_done, 4)
            pe.sem_inc(s_done, 1)
            pe.sem_inc(pv_done, 2)
            pe.sem_inc(t1_done, CH)
            pe.sem_inc(at_done, 2)
            pe.wait_ge(consts_in, 16 * NCONST)

            def transposes(b):
                pe.wait_ge(xn_ready, b + 1)
                pe.wait_ge(xT_ready, 4 * b + 4)
                for n in range(4):
                    half, k = divmod(n, 2)
                    for j in range(BANK // P):
                        ins = nc.tensor.transpose(bank(n)[:, j * P:(j + 1) * P],
                                                  xnb[:, half * (BANK // P) + j, k * P:(k + 1) * P], idf[:, :])
                    ins.then_inc(xpose_done, 1)

            def batch(b, last):
                for i, (n, c) in enumerate(PROJ):
                    side, m = SIDES[n]
                    pe.wait_ge(xT_ready, 4 * b + 6 + 2 * c)
                    pe.wait_ge(proj_out, 8 * b + i + 1)
                    for k in range(KT):
                        ins = nc.tensor.matmul(bank(4 + i % 2), (wk_sb, wq_sb)[side][:, k, m * P:(m + 1) * P],
                                               xnT[:, k, c * BANK:(c + 1) * BANK],
                                               start=(k == 0), stop=(k == KT - 1))
                    ins.then_inc(proj_done, 1)
                if not last:
                    transposes(b + 1)
                for t in range(TB):
                    pe.wait_ge(v_out, TB * b + t + 1)
                    for k in range(KT):
                        ins = nc.tensor.matmul(bank(6 + t % 2)[:, 0:D + E], xnT[:, k, t * P:(t + 1) * P],
                                               wvg_sb[:, k, :], start=(k == 0), stop=(k == KT - 1))
                    ins.then_inc(v_done, 1)

            transposes(0)
            with pe.Fori(0, B - 1) as b:
                batch(b, False)
            batch(B - 1, True)

            pe.wait_ge(picked, 1)
            for n in range(2):
                ins = nc.tensor.matmul(bank(6 + n)[:, 0:NT * E], before_sb[:, n * P:(n + 1) * P],
                                       picked_b[:, :, :].rearrange("p t e -> p (t e)"), start=True, stop=True)
            ins.then_inc(counted, 1)

            def score_piece(i, n, piece):
                ib, seg, width, h0, heads = piece
                diagonal = seg + width == P * (ib + 1)
                for h in range(heads):
                    out_ = bank(i % 2)[:, h * width:(h + 1) * width]
                    ins = nc.tensor.matmul(out_, k_aug[n][0:SCORE_ROWS, h0 + h, ib * P:(ib + 1) * P],
                                           q_aug[n][0:SCORE_ROWS, h0 + h, seg:seg + width],
                                           start=True, stop=not diagonal)
                    if diagonal:
                        ins = nc.tensor.matmul(out_[:, width - P:width], idb[:, :], mask_sb[:, :],
                                               start=False, stop=True)
                return ins

            def send_piece(base, i, n):
                pe.wait_ge(piece_used, base + i + 1)
                score_piece(i, n, PIECES[i]).then_inc(piece_done, 1)

            def send_maxima(q, base):
                pe.wait_ge(m_split, q + 1)
                pe.wait_ge(piece_used, base + NP + 1)
                nc.tensor.transpose(bank(NP % 2).bitcast(bf16)[0:NSPLIT * TB * HQ, 0:P], msplit[:, :],
                                    idb[:, :]).then_inc(piece_done, 1)

            def send_outputs(q, base):
                pe.wait_ge(o_out, q + 2)
                for half in range(2):
                    pe.wait_ge(piece_used, base + half + 1)
                    for j in range(TB // 2):
                        i = half * TB // 2 + j
                        ins = nc.tensor.transpose(bank(half)[:, j * P:(j + 1) * P],
                                                  oT[:, i * P:(i + 1) * P], idf[:, :])
                    ins.then_inc(piece_done, 1)

            def unit_scores(n, i, unit):
                base = (2 + 2 * (i % 2)) * BANK
                for jb, h, col0 in unit:
                    columns = q_aug[n][0:ALL_ROWS, h, jb * P:(jb + 1) * P]
                    lo, i0 = col0, P * jb
                    end = col0 + T - P * jb
                    while lo < end:
                        hi = min(end, (lo // BANK + 1) * BANK)
                        ins = nc.tensor.matmul(ps[:, base + lo:base + hi], columns,
                                               k_aug[n][0:ALL_ROWS, h, i0:i0 + hi - lo],
                                               start=True, stop=lo > col0)
                        if lo == col0:
                            ins = nc.tensor.matmul(ps[:, base + lo:base + lo + P], idb[:, :], maskT_sb[:, :],
                                                   start=False, stop=True)
                        i0 += hi - lo
                        lo = hi
                return ins

            def group_outputs(n, k, jb, c):
                lo, hi = max(P * jb, c * BANK), (c + 1) * BANK
                last = jb == (TB // 2 - 1 if c == 0 else TB // 2)
                for u, unit in enumerate(TYPES[k]):
                    for part, h, col0 in unit:
                        if part == jb:
                            at_ = col0 + lo - P * jb
                            ins = nc.tensor.matmul(ps[2 * HD * h:2 * HD * (h + 1), 6 * BANK + lo:6 * BANK + hi],
                                                   v_q[n][:, jb, h, :], probs[SLOT[k, u]][:, at_:at_ + hi - lo],
                                                   start=(jb == 0), stop=last)
                return ins

            def send_group(q, n, g):
                k, jb, c = GROUPS[g]
                if g == 0:
                    pe.wait_ge(vq_ready, q + 1)
                    pe.wait_ge(o_out, q + 1)
                if g == 0 or GROUPS[g - 1][0] != k:
                    pe.wait_ge(exp_done, NU * q + LAST_OF_TYPE[k] + 2)
                ins = group_outputs(n, k, jb, c)
                if g + 1 == len(GROUPS) or GROUPS[g + 1][0] != k:
                    ins.then_inc(pv_done, 1)

            def window(q, n, first=False, last=False):
                base = PRO + WIN * q
                sent = done = 0
                pe.wait_ge(m_in, 48 * q + 48)
                for i, (k, u, unit) in enumerate(UNITS):
                    pe.wait_ge(exp_done, NU * q + i + 1)
                    unit_scores(n, i, unit).then_inc(s_done, 1)
                    if i == 1 and not first:
                        send_outputs(q - 1, base - 2)
                    if i == 1 and not last:
                        pe.wait_ge(aug_in[(n + 1) % AUG], 192 * next_round(q) + 192)
                    if i >= 1 and not last:
                        upto = min(NP, -(-NP * i // SPREAD))
                        for piece in range(sent, upto):
                            send_piece(base, piece, (n + 1) % AUG)
                        sent = upto
                    if done < len(GROUPS) and LAST_OF_TYPE[GROUPS[done][0]] + LAG <= i + 1:
                        send_group(q, n, done)
                        done += 1
                if not last:
                    send_maxima(q + 1, base)
                for g in range(done, len(GROUPS)):
                    send_group(q, n, g)

            pe.wait_ge(aug_in[0], 192)
            for i in range(NP):
                send_piece(0, i, 0)
            send_maxima(0, 0)
            pe.wait_ge(ones_set, AUG)

            in_loop = [None]

            def next_round(q):
                if isinstance(q, int):
                    return (q + 1) // AUG
                t, r = in_loop[0]
                return t + (r + 2) // AUG

            window(0, 0, first=True)
            with pe.Fori(0, ROUNDS) as t:
                for r in range(AUG):
                    in_loop[0] = (t, r)
                    window(AUG * t + r + 1, (r + 1) % AUG)
            for q in range(FIRST_TAIL, NQ):
                window(q, q % AUG, last=q == NQ - 1)
            send_outputs(NQ - 1, PRO + WIN * (NQ - 1))
            pe.wait_ge(piece_used, PRO + WIN * (NQ - 1) + 4)
            pe.wait_ge(o_out, NQ + 1)
            pe.wait_ge(moe_w_in, 64)

            def x_transpose(n, j):
                pe.wait_ge(xg_in[j % CH], 16 * rnd_of(n, j) + 16)
                pe.wait_ge(xgT_out, n + 1)
                for k in range(KT):
                    ins = nc.tensor.transpose(bank(j % 2)[:, k * P:(k + 1) * P], xg[j % CH][:, k * P:(k + 1) * P],
                                              idf[:, :])
                ins.then_inc(t1_done, 1)

            def layer(n, w, xT, out_):
                pe.sem_inc(passed, 1)
                e = pe.value_load(tile_expert[0:1, bass.ds(n, 1)], min_val=0, max_val=E - 1)
                for k in range(KT):
                    ins = nc.tensor.matmul(out_, xT[:, k * P:(k + 1) * P], w[:, e * KT + k, :],
                                           start=(k == 0), stop=(k == KT - 1))
                return ins

            def hidden(n, j):
                pe.wait_ge(xgT_out, n + 3)
                pe.wait_ge(h_out, n + 1)
                layer(n, w1_sb, xgT[j % 2], bank(2 + j % 2)[:, 0:D]).then_inc(l1_done, 1)

            def g_transpose(n, j):
                pe.wait_ge(g_done, n + 1)
                pe.wait_ge(gT_out, n + 1)
                for k in range(KT):
                    ins = nc.tensor.transpose(bank(4 + j % 2)[:, k * P:(k + 1) * P], hid[j % 2][:, k * P:(k + 1) * P],
                                              idf[:, :])
                ins.then_inc(t2_done, 1)

            def expert_out(n, j):
                pe.wait_ge(gT_out, n + 3)
                pe.wait_ge(y_out, n + 1)
                layer(n, w2_sb, hidT[j % 2], bank(6 + j % 2)[:, 0:D]).then_inc(l2_done, 1)

            skewed(pe, ((x_transpose, 3), (hidden, 2), (g_transpose, 1), (expert_out, 0)))

            pe.wait_ge(y_out, SLOTS + 2)
            with pe.Fori(0, NT // 4) as t:
                for par in range(2):
                    n = 2 * t + par
                    pe.wait_ge(a_in[par], 32 * t + 32)
                    pe.wait_ge(at_out, n + 1)
                    for s in range(2 * KT):
                        ins = nc.tensor.transpose(bank(4 * par)[:, s * P:(s + 1) * P],
                                                  a_tok[par][:, s * P:(s + 1) * P], idf[:, :])
                    ins.then_inc(at_done, 1)
                    pe.wait_ge(at_out, n + 3)
                    pe.wait_ge(sg_used, n + 1)
                    for j in range(2):
                        for k in range(KT):
                            s = j * KT + k
                            ins = nc.tensor.matmul(bank(4 * par + 2)[:, j * D:(j + 1) * D],
                                                   aT[par][:, s * P:(s + 1) * P], wo_sb[:, k, :],
                                                   start=(k == 0), stop=(k == KT - 1))
                    ins.then_inc(sg_done, 1)


def kernel(**inputs):
    import numpy as np
    import concourse.bacc as bacc
    from concourse.bass_utils import run_bass_kernel_spmd

    def rows(n, m):
        return np.ascontiguousarray(np.broadcast_to(n, (m,) + n.shape))

    def block_(name):
        return np.asarray(inputs[name])

    bf = mybir.dt.np(bf16)
    pos = np.arange(T)
    tile, within = pos // P, pos % P
    border = np.arange(1, TB)[:, None]
    k_rows = np.concatenate([(tile[None] >= border).astype(np.float32), -within[None], np.ones((1, T))])
    q_rows = np.concatenate([-P * (tile[None] < border).astype(np.float32), np.ones((1, T)), within[None],
                             -np.ones((NSPLIT, T))])
    heads = lambda a: np.ascontiguousarray(np.broadcast_to(a[:, None, :], (a.shape[0], HQ, T))).astype(bf)
    low = np.tril(np.ones((P, P), bool))
    ahead = np.tril(np.ones((E, E)), -1).reshape(-1)
    shape_numbers = np.concatenate([np.arange(E), P * np.arange(NT), ahead, np.arange(SLOTS)])
    numbers = np.concatenate([rows(shape_numbers, P), P * np.arange(NT)[None] + np.arange(P)[:, None]], axis=1)
    args = {
        "x": block_("L0_attn_x"),
        "wqT": block_("L0_attn_q_w").T,
        "wkT": block_("L0_attn_k_w").T,
        "wvT": block_("L0_attn_v_w").T,
        "woT": block_("L0_attn_o_w").T,
        "qb": block_("L0_attn_q_b").reshape(KT, P).T,
        "kb": block_("L0_attn_k_b").reshape(KT, P).T,
        "vb": rows(block_("L0_attn_v_b"), P),
        "ob": rows(block_("L0_attn_o_b"), P),
        "gate": block_("L0_ffn_gate_w"),
        "w1": block_("L0_ffn_fc1_w"),
        "b1": rows(block_("L0_ffn_fc1_b"), P),
        "w2": block_("L0_ffn_fc2_w"),
        "b2": rows(block_("L0_ffn_fc2_b"), P),
        "alpha": rows(block_("L0_ffn_alpha"), P),
        "ident_f": np.eye(P, dtype=np.float32),
        "ident_b": np.eye(P).astype(bf),
        "mask_neg": np.where(low, 0.0, NEG).astype(bf),
        "mask_negT": np.where(low.T, 0.0, NEG).astype(bf),
        "before": np.concatenate([np.triu(np.ones((P, P)), 1), np.ones((P, P))], axis=1).astype(bf),
        "k_rows": heads(k_rows),
        "q_rows": heads(q_rows),
        "numbers": numbers.astype(np.float32),
    }
    nc = bacc.Bacc("TRN2", target_bir_lowering=False, num_devices=1)
    arrays, aps = {}, []
    for name, a in args.items():
        a = np.ascontiguousarray(a)
        arrays[f"in_{name}"] = a
        aps.append(nc.dram_tensor(f"in_{name}", a.shape, mybir.dt.from_np(a.dtype), kind="ExternalInput").ap())
    out = nc.dram_tensor("out", (B, T, D), fp32, kind="ExternalOutput").ap()
    attention_moe_kernel(nc, *aps, out)
    r = run_bass_kernel_spmd(nc, [arrays], core_ids=[0])
    return r.results[0]["out"]
```

```python
import concourse.bass as bass
from concourse import mybir
from contextlib import ExitStack

fp32 = mybir.dt.float32
bf16 = mybir.dt.bfloat16
i32 = mybir.dt.int32
ALU = mybir.AluOpType
ACT = mybir.ActivationFunctionType
AX = mybir.AxisListType

P = 128
B, T, D = 4, 1024, 256
H, HD = 16, 16
E = 8
KT = D // P
TB = T // P
NT = B * TB
HQ = 4
NQ = B * H // HQ
QF = HQ * HD
SCALE = HD ** -0.5
EPS = 1e-5
NEG = -3.0e38
BANK = 512

K_PART = (0, 0, 1, 1, 0, 2)
Q_PART = (0, 1, 0, 1, 2, 0)
NSPLIT = 3
DATA_ROWS = len(K_PART) * HD
DECAY_ROWS = (TB - 1) + 2
SCORE_ROWS = DATA_ROWS + DECAY_ROWS
ALL_ROWS = SCORE_ROWS + NSPLIT

PIECES = []
for ib in range(TB):
    pitch = P * (ib + 1) if ib < 2 else BANK if ib < 4 else 2 * BANK
    heads = 2 if ib == 0 else min(HQ, 2 * BANK // pitch)
    PIECES += [(ib, h, heads, pitch) for h in range(0, HQ, heads)]
NP = len(PIECES)
TYPES = [[[(0, h, 0)] for h in range(HQ)]]
for jb in range(1, TB // 2):
    TYPES.append([[(jb, h, 0), (TB - jb, h, T - P * jb)] for h in range(HQ)])
TYPES.append([[(TB // 2, h, 0), (TB // 2, h + 1, T // 2)] for h in range(0, HQ, 2)])
NTY = len(TYPES)
UNITS = [(k, n, parts) for k, units in enumerate(TYPES) for n, parts in enumerate(units)]
NU = 2 * len(UNITS)
LAST_OF_TYPE = [2 * sum(len(u) for u in TYPES[:k + 1]) for k in range(NTY)]
SLOT = {(k, u): HQ * (k % 2) + ((u + 2) % HQ if k == 0 else u) for k, u, _ in UNITS}
NSLOT = 2 * HQ
GROUPS = [(k, jb, c) for k in range(NTY) for jb in sorted({p[0] for u in TYPES[k] for p in u})
          for c in range(2) if P * jb < (c + 1) * BANK]
GROUP_STEP = (10, 12, 17, 19, 21, 25, 27, 29, 33, 35, NU + 1, NU + 3)
COUNT_STEP = 7
EVACUATE = 5
AHEAD = 8
AHEAD_OF_MAXIMA = 3
EXPERTS_ITEM = 16
INVERT_ITEM = 9


def stream(ahead, more=2):
    items = [("piece", ahead, i) for i in range(AHEAD if ahead else 0, NP)]
    items += [("piece", ahead + 1, i) for i in range(AHEAD_OF_MAXIMA)] + [("maxima", ahead, 0)]
    items += [("piece", ahead + 1, i) for i in range(AHEAD_OF_MAXIMA, AHEAD)]
    return [item for item in items if item[1] <= more]


PRO = len(stream(0))
SKIP = 7
WIN = len(stream(1))
assert WIN % 2 == 0 and WIN == NU - len(GROUP_STEP)
AUG = 3
ROUNDS = 4
FIRST_TAIL = 1 + AUG * ROUNDS
LAST_ITEM = PRO + WIN * (NQ - 2) + len(stream(1, more=1))

SLOTS = (2 * B * T + E * (P - 1)) // P
SLOTS += -SLOTS % 8
CH = 4
STEP = 2 * CH
ST = NT // (2 * ROUNDS)


CT = BANK // P
CHUNKS = 2
assert CHUNKS * CT == TB
PLAIN = 2
WEIGHTS = ("wk", "wq", "qb", "kb", "vb", "wv", "gate")
CONSTS = ("idb", "mask", "maskT", "before", "num", "alpha", "wo", "ob")
NCONST = len(CONSTS) + 2 * AUG
DEEP = 4
PAIRS = TB // 2
assert DEEP == PAIRS


def rnd_of(n, j):
    return n // CH if isinstance(n, int) else LOOP_ROUND[0] * (STEP // CH) + j // CH


LOOP_ROUND = [None]


def skewed(eng, stages):
    def straight(tiles):
        for n in tiles:
            for what, ahead in stages:
                if 0 <= n + ahead < SLOTS:
                    what(n + ahead, n + ahead)

    straight(range(-CH, STEP))
    with eng.Fori(1, SLOTS // STEP - 1) as t:
        LOOP_ROUND[0] = t
        for j in range(STEP):
            for what, ahead in stages:
                what(STEP * t + j + ahead, j + ahead)
    straight(range(SLOTS - STEP, SLOTS))


def items_at(i, n):
    steps = 8 * CHUNKS * (B - PLAIN)
    at = 8 * i + n
    count = lambda k: max(0, -(-(k - SKIP) * PRO // (steps - SKIP)))
    return count(at + 1) - count(at)


def is_last(q):
    return isinstance(q, int) and q == NQ - 1


def in_turn(eng, ahead, what):
    ahead(0, 0)
    with eng.Fori(0, B - 1) as t:
        for j in range(PAIRS):
            ahead(t + (j + 1) // PAIRS, (j + 1) % PAIRS)
            what(t, j)
    for j in range(PAIRS):
        if j + 1 < PAIRS:
            ahead(B - 1, j + 1)
        what(B - 1, j)


def attention_moe_kernel(nc, x, wqT, wkT, wvT, woT, qb, kb, vb, ob, gate, w1, b1, w2, b2, alpha,
                         ident_f, ident_b, mask_neg, mask_negT, before, k_rows, q_rows, numbers, empty_rows, out):
    x_t = x.rearrange("b (t p) d -> p (b t) d", p=P)
    out_t = out.rearrange("b (t p) d -> p (b t) d", p=P)

    ctx = ExitStack()
    with ctx:
        def sb(name, shape, dt=fp32):
            return ctx.enter_context(nc.sbuf_tensor(name, shape, dt))

        def sem(name):
            return ctx.enter_context(nc.semaphore(name))

        k_parts = nc.dram_tensor("k_parts", [NSPLIT, NQ * QF, T], bf16).ap()
        q_parts = nc.dram_tensor("q_parts", [NSPLIT, NQ * QF, T], bf16).ap()
        xn_dram = nc.dram_tensor("xn_dram", [B * T, D], fp32).ap()
        a_dram = nc.dram_tensor("a_dram", [B * D, T], fp32).ap()
        inv_dram = nc.dram_tensor("inv_dram", [NQ * HQ, T], fp32).ap()
        slot_dram = nc.dram_tensor("slot_dram", [P * SLOTS, 1], i32).ap()
        xs_dram = nc.dram_tensor("xs_dram", [SLOTS * P, D], fp32).ap()
        y_dram = nc.dram_tensor("y_dram", [2 * B * T + SLOTS * P, D], fp32).ap()
        xn_t = xn_dram.rearrange("(t p) d -> p t d", p=P)
        xs_t = xs_dram.rearrange("(n p) d -> p n d", p=P)
        a_f = a_dram.rearrange("(b k p) t -> p b k t", k=KT, p=P)
        y_t = y_dram[0:2 * B * T, :].rearrange("(t p k) d -> p t (k d)", p=P, k=2)

        wq_sb = sb("wq_sb", [P, KT, D])
        wk_sb = sb("wk_sb", [P, KT, D])
        wvg_sb = sb("wvg_sb", [P, KT, D + E])
        wo_sb = sb("wo_sb", [P, KT, D])
        qb_sb = sb("qb_sb", [P, KT])
        kb_sb = sb("kb_sb", [P, KT])
        kbs_sb = sb("kbs_sb", [P, KT])
        vb_sb = sb("vb_sb", [P, D])
        ob_sb = sb("ob_sb", [P, D])
        w1_sb = sb("w1_sb", [P, E * KT, D])
        w2_sb = sb("w2_sb", [P, E * KT, D])
        alpha_sb = sb("alpha_sb", [P, E])
        num_sb = sb("num_sb", [P, numbers.shape[1]])
        idf = sb("idf", [P, P])
        idb = sb("idb", [P, P], bf16)
        mask_sb = sb("mask_sb", [P, P], bf16)
        maskT_sb = sb("maskT_sb", [P, P], bf16)
        before_sb = sb("before_sb", [P, 2 * P], bf16)
        v_all = sb("v_all", [P, NQ, TB, QF])
        logits = sb("logits", [P, NT, E])
        weight = sb("weight", [P, NT, 2])
        slot = sb("slot", [P, NT, 2], i32)
        tile_expert = sb("tile_expert", [P, SLOTS], i32)
        y_row_of = sb("y_row_of", [P, SLOTS], i32)
        y_row = sb("y_row", [P, NT, 2], i32)
        slot_now = sb("slot_now", [P, ST, 2], i32)
        y_row_now = sb("y_row_now", [P, ST, 2], i32)
        y_rows = sb("y_rows", [P, CH], i32)
        zeros = sb("zeros", [P, D])
        picked_b = sb("picked_b", [P, NT, E], bf16)
        ARENA = 16 * 1024
        arena = sb("arena", [P, ARENA])
        at = [0]

        def cut(cols, dt=fp32):
            words = cols if dt == fp32 else cols // 2
            a = arena[:, at[0]:at[0] + words]
            at[0] += words
            assert at[0] <= ARENA
            return a if dt == fp32 else a.bitcast(dt)

        def cut_parts():
            return [cut(NSPLIT * BANK, bf16).rearrange("p (s t) -> p s t", s=NSPLIT) for _ in range(4)]

        parts = [cut_parts()]
        xnT = [cut(KT * BANK).rearrange("p (k t) -> p k t", k=KT) for _ in range(CHUNKS)]
        last_parts = at[0]
        parts += [cut_parts()]
        after_probs = at[0]
        xb = [cut(CT * D).rearrange("p (t d) -> p t d", d=D) for _ in range(CHUNKS)]
        xnb = [cut(CT * D).rearrange("p (t d) -> p t d", d=D) for _ in range(CHUNKS)]
        whole = [[cut(BANK) for _ in range(4)] for _ in range(CHUNKS)]
        at[0] = after_probs
        gat = [cut(NT * E).rearrange("p (t e) -> p t e", e=E) for _ in range(6)]
        ahead_in, of_tile = [cut(NT * E).rearrange("p (t e) -> p t e", e=E) for _ in range(2)]
        col = [cut(NT) for _ in range(8)]
        need = cut(E * NT).rearrange("p (e k) -> p e k", e=E)
        ahead = cut(E * E).rearrange("p (e f) -> p e f", e=E)
        full = cut(SLOTS * (E - 1)).rearrange("p (n e) -> p n e", e=E - 1)
        some = [cut(E) for _ in range(3)]
        expert_f = cut(SLOTS)
        tiles, base, upto = some
        upto_tile = gat[5]
        slot_f = cut(NT * 2).rearrange("p (t k) -> p t k", k=2)
        assert at[0] <= after_probs + 2 * CHUNKS * CT * D
        at[0] = 0
        probs = [cut(T) for _ in range(NSLOT)]
        assert at[0] == after_probs and HQ * T <= last_parts
        oT = cut(T)
        inverse = cut(T)
        o_norm = cut(T)
        x_move = cut(ST * D).rearrange("p (t d) -> p t d", d=D)
        assert at[0] <= ARENA - 2 * E * D
        at[0] = ARENA - 2 * E * D
        b1_sb = cut(E * D).rearrange("p (e n) -> p e n", e=E)
        b2_sb = cut(E * D).rearrange("p (e n) -> p e n", e=E)
        at[0] = 0
        xg = [x_move[:, j, :] for j in range(CH)]
        assert ST >= CH
        xgT = [cut(D) for _ in range(CH)]
        hid = [cut(D) for _ in range(CH)]
        w1_now = [cut(KT * D).rearrange("p (k n) -> p k n", k=KT) for _ in range(2)]
        ysb = [cut(D) for _ in range(CH)]
        at[0] = after_moe = max(at[0], DEEP * 4 * D)
        aT = [cut(2 * D).rearrange("p (k t) -> p k t", k=KT) for _ in range(DEEP)]
        assert at[0] <= ARENA - 2 * E * D
        ya = [cut(4 * D).rearrange("p (t k d) -> p t k d", t=2, k=2) for _ in range(DEEP)]
        at[0] = 0
        gsum = [cut(2 * D) for _ in range(DEEP)]
        so = [cut(2 * D) for _ in range(DEEP)]
        assert at[0] <= after_moe

        aug = sb("aug", [P, 2 * AUG, HQ, T], bf16)
        k_aug = [aug[:, n, :, :] for n in range(AUG)]
        q_aug = [aug[:, AUG + n, :, :] for n in range(AUG)]
        x_all = aug[:, :, :, :].rearrange("p a h t -> p (a h t)").bitcast(fp32)[:, 0:NT * D]
        x_all = x_all.rearrange("p (t d) -> p t d", d=D)
        a_all = v_all[:, :, :, :].rearrange("p q t f -> p (q t f)").rearrange("p (b k t) -> p b k t", b=B, k=KT)
        v_q = [sb(f"v_q{n}", [P, TB, HQ, 2 * HD]) for n in range(AUG)]
        sums = sb("sums", [P, HQ * T // P])
        mxa = sb("mxa", [P, HQ, TB])
        mrest = sb("mrest", [P, HQ, TB])
        msplit = sb("msplit", [P, NSPLIT * TB * HQ], bf16)
        mT = sb("mT", [NSPLIT * TB * HQ, P], bf16)
        stats = sb("stats", [P, CHUNKS, CT, 6])
        mv = sb("mv", [P, CHUNKS, CT, 2])
        veps = sb("veps", [P, CT])
        std = sb("std", [P, CT])
        rstd = sb("rstd", [P, CHUNKS, CT])

        ps = ctx.enter_context(nc.psum_tensor("ps", [P, 8 * BANK], fp32))

        def bank(n, k=1):
            return ps[:, n * BANK:(n + k) * BANK]

        def pair(base, i):
            return bank(2 * (((base if isinstance(base, int) else PRO) + i) % 2), 2)

        def score_bank(q, i):
            return bank(i % 6) if is_last(q) else bank(4 + i % 2)

        ident_in = sem("ident_in"); weights_in = sem("weights_in"); consts_in = sem("consts_in")
        bias_ready = sem("bias_ready")
        x_in = [sem(f"x_in{c}") for c in range(CHUNKS)]; rstd_ready = sem("rstd_ready")
        var_ready = sem("var_ready"); std_ready = sem("std_ready"); xn_ready = sem("xn_ready")
        xn_out = [sem(f"xn_out{c}") for c in range(CHUNKS)]
        xpose_done = sem("xpose_done"); xT_ready = sem("xT_ready")
        proj_done = sem("proj_done"); proj_out = sem("proj_out"); split_done = sem("split_done")
        parts_out = [sem(f"parts_out{c}") for c in range(CHUNKS)]
        v_done = sem("v_done"); v_out = sem("v_out")
        ln_step = sem("ln_step"); split_step = sem("split_step"); gate_step = sem("gate_step")
        m_step = sem("m_step")
        passed = sem("passed")
        gap_ready = sem("gap_ready"); gexp_ready = sem("gexp_ready")
        picked = sem("picked"); counted = sem("counted"); counts_out = sem("counts_out"); shares_ready = sem("shares_ready")
        route_step = sem("route_step"); summed = sem("summed"); bases_ready = sem("bases_ready"); routed = sem("routed")
        zeros_set = sem("zeros_set"); xs_zero = sem("xs_zero"); table_out = sem("table_out")
        rows_ready = sem("rows_ready"); x_moved = sem("x_moved"); scattered = sem("scattered")
        table_in = sem("table_in")
        moe_w_in = sem("moe_w_in")
        ones_set = sem("ones_set"); vq_ready = sem("vq_ready")
        aug_in = [sem(f"aug_in{n}") for n in range(AUG)]
        piece_done = sem("piece_done"); piece_used = sem("piece_used")
        m_split = sem("m_split"); mT_ready = sem("mT_ready"); m_in = sem("m_in")
        s_done = sem("s_done"); exp_done = sem("exp_done")
        pv_done = sem("pv_done"); o_out = sem("o_out")
        sums_set = sem("sums_set"); sums_in = sem("sums_in"); inverse_ready = sem("inverse_ready")
        inverse_out = sem("inverse_out"); inverse_in = sem("inverse_in")
        o_normed = sem("o_normed"); a_stored = sem("a_stored")
        y_rows_ready = sem("y_rows_ready"); xg_in = [sem(f"xg_in{n}") for n in range(CH)]
        t1_done = sem("t1_done"); xgT_out = sem("xgT_out"); l1_done = sem("l1_done"); h_out = sem("h_out")
        g_done = sem("g_done"); w1_ready = sem("w1_ready"); l2_done = sem("l2_done")
        y_out = sem("y_out"); y_stored = [sem(f"y_stored{n}") for n in range(CH)]
        x_all_in = sem("x_all_in"); a_in = sem("a_in"); aT_ready = sem("aT_ready")
        ya_in = [sem(f"ya_in{n}") for n in range(DEEP)]
        s_proj = sem("s_proj"); s_used = sem("s_used"); y_scaled = sem("y_scaled")
        gsum_done = sem("gsum_done"); silu_done = sem("silu_done"); sg_done = sem("sg_done")
        fin_done = sem("fin_done"); stored = sem("stored")

        SIDES = [(side, m) for side in range(2) for m in range(KT)]

        e_index = num_sb[:, 0:E]
        at_num = E
        multiples = num_sb[:, at_num:at_num + NT]
        at_num += NT
        is_ahead = num_sb[:, at_num:at_num + E * E].rearrange("p (e f) -> p e f", e=E)
        at_num += E * E
        tile_index = num_sb[:, at_num:at_num + SLOTS]
        at_num += SLOTS
        y_row_f = num_sb[:, at_num:at_num + 2 * NT]
        at_num += 2 * NT
        assert at_num == numbers.shape[1]

        def spread(ap, n):
            return bass.AP(ap.tensor, ap.offset, [list(x) for x in ap.ap] + [[0, n]])

        def over(ap, n):
            return bass.AP(ap.tensor, ap.offset, [list(ap.ap[0]), [0, n]] + [list(x) for x in ap.ap[1:]])

        def many_zeros(n):
            return bass.AP(zeros[:, :].tensor, zeros[:, :].offset,
                           [list(zeros[:, :].ap[0]), [0, n], [1, D]])

        best, first, second, gap, gexp, where, norm, low = col

        block = ctx.enter_context(nc.Block())

        @block.sync
        def _(sp):
            for c in range(CHUNKS):
                sp.sem_inc(parts_out[c], 16 * 4)
                sp.sem_inc(xn_out[c], 16)
            sp.sem_inc(a_stored, 16 * HQ)
            def load_x_chunk(b, c):
                sp.dma_start(xb[c], x_t[:, bass.ds(TB * b + CT * c, CT), :]).then_inc(x_in[c], 16)

            weights = lambda w: w.rearrange("(k p) n -> p k n", p=P)
            load_x_chunk(0, 0)
            sp.dma_start(idf[:, :], ident_f).then_inc(ident_in, 16)
            loads = {"wk": (wk_sb[:, :, :], weights(wkT)), "wq": (wq_sb[:, :, :], weights(wqT)),
                     "qb": (qb_sb[:, :], qb), "kb": (kb_sb[:, :], kb), "vb": (vb_sb[:, :], vb),
                     "wv": (wvg_sb[:, :, 0:D], weights(wvT)), "gate": (wvg_sb[:, :, D:D + E], weights(gate)),
                     "idb": (idb[:, :], ident_b), "mask": (mask_sb[:, :], mask_neg),
                     "maskT": (maskT_sb[:, :], mask_negT), "before": (before_sb[:, :], before),
                     "num": (num_sb[:, :], numbers), "alpha": (alpha_sb[:, :], alpha),
                     "wo": (wo_sb[:, :, :], weights(woT)), "ob": (ob_sb[:, :], ob)}
            for name in WEIGHTS:
                sp.dma_start(*loads[name]).then_inc(weights_in, 16)
            load_x_chunk(0, 1)
            for name in CONSTS:
                sp.dma_start(*loads[name]).then_inc(consts_in, 16)
            for n in range(AUG):
                sp.dma_start(k_aug[n][DATA_ROWS:SCORE_ROWS], k_rows).then_inc(consts_in, 16)
                sp.dma_start(q_aug[n][DATA_ROWS:ALL_ROWS], q_rows).then_inc(consts_in, 16)
            sp.dma_start(slot_dram, empty_rows).then_inc(table_out, 16)

            def store_normalised(i, b, c):
                sp.wait_ge(xn_ready, i + 1)
                sp.dma_start(xn_t[:, bass.ds(TB * b + CT * c, CT), :], xnb[c]).then_inc(xn_out[c], 16)

            def chunk(b, c, more=B * CHUNKS):
                i = CHUNKS * b + c
                for n, (side, m) in enumerate(SIDES):
                    sp.wait_ge(split_done, 4 * i + n + 9)
                    dst = (k_parts, q_parts)[side]
                    sp.dma_start(dst[:, bass.ds(b * D + m * P, P), c * BANK:(c + 1) * BANK].rearrange("s p t -> p s t"),
                                 parts[c][n]).then_inc(parts_out[c], 16)
                    if n == 2 and more == 0:
                        load_maxima(0, 0)
                    if n == 0 and more > 0:
                        store_normalised(i + 1, b + c, 1 - c)
                        if more > 2:
                            load_x_chunk(b + c + 1, 1 - c)

            store_normalised(0, 0, 0)
            load_x_chunk(1, 0)

            def load_quad(q, n):
                for g in range(len(K_PART)):
                    rows = slice(HD * g, HD * (g + 1))
                    for aug, src, part in ((k_aug, k_parts, K_PART[g]), (q_aug, q_parts, Q_PART[g])):
                        sp.dma_start(aug[n][rows, :, :],
                                     src[part, bass.ts(q, QF), :].rearrange("(h d) t -> d h t", d=HD)
                                     ).then_inc(aug_in[n], 16)

            def load_maxima(q, n):
                sp.wait_ge(mT_ready, q + 1)
                for s in range(NSPLIT):
                    dst = k_aug[n][SCORE_ROWS + s:SCORE_ROWS + s + 1, :, :]
                    rows = mT[s * TB * HQ:(s + 1) * TB * HQ, :]
                    sp.dma_start(dst.rearrange("o h (t i) -> o (h t) i", t=TB), rows).then_inc(m_in, 16)

            def spread_sums(q):
                sp.wait_ge(o_out, q + 2)
                for h in range(HQ):
                    row = 2 * HD * h + HD
                    sp.dma_start(sums[h * P // HQ:(h + 1) * P // HQ, :],
                                 oT[row:row + 1, :].rearrange("o (s w) -> o s w", s=P // HQ)).then_inc(sums_in, 16)

            def store_inverses(q):
                sp.wait_ge(inverse_ready, q + 1)
                for h in range(HQ):
                    sp.dma_start(inv_dram[bass.ds(HQ * q + h, 1), :].rearrange("o (s w) -> o s w", s=P // HQ),
                                 sums[h * P // HQ:(h + 1) * P // HQ, :]).then_inc(inverse_out, 16)

            def load_inverses(q):
                sp.wait_ge(inverse_out, 16 * HQ * q + 16 * HQ)
                sp.wait_ge(o_normed, q + 1)
                for h in range(HQ):
                    row = inv_dram[bass.ds(HQ * q + h, 1), :]
                    sp.dma_start(inverse[2 * HD * h:2 * HD * h + HD, :],
                                 bass.AP(row.tensor, row.offset, [[0, HD], [1, T]])).then_inc(inverse_in, 16)

            def store_quad(q):
                sp.wait_ge(o_normed, q + 2)
                for h in range(HQ):
                    sp.dma_start(a_dram[bass.ds(QF * q + HD * h, HD), :],
                                 o_norm[2 * HD * h:2 * HD * h + HD, :]).then_inc(a_stored, 16)

            with sp.Fori(0, PLAIN) as b:
                for c in range(CHUNKS):
                    chunk(b, c)
            for c in range(CHUNKS):
                sp.wait_ge(parts_out[c], 16 * 4 * 2)
            load_quad(0, 0)
            load_quad(1, 1)
            for b in range(PLAIN, B):
                for c in range(CHUNKS):
                    chunk(b, c, (B - b) * CHUNKS - c - 1)
            for c in range(CHUNKS):
                sp.wait_ge(parts_out[c], 16 * 4 * (B + 1))

            def window(q, n):
                if not isinstance(q, int) or q + 2 < NQ:
                    sp.wait_ge(s_done, NU * q + 1)
                    load_quad(q + 2, (n + 2) % AUG)
                if not isinstance(q, int) or q > 0:
                    spread_sums(q - 1)
                    store_inverses(q - 1)
                    load_inverses(q - 1)
                if not isinstance(q, int) or q + 1 < NQ:
                    load_maxima(q + 1, (n + 1) % AUG)
                if not isinstance(q, int) or q > 0:
                    store_quad(q - 1)

            window(0, 0)
            sp.wait_ge(sums_set, 1)
            with sp.Fori(0, ROUNDS) as t:
                for r in range(AUG):
                    window(AUG * t + r + 1, (r + 1) % AUG)
                    per = E // ROUNDS
                    if r < per:
                        for dst, src in ((w1_sb, w1), (w2_sb, w2)):
                            sp.dma_start(dst[:, bass.ds((per * t + r) * KT, KT), :],
                                         src[per * t + r, :, :].rearrange("(k p) n -> p k n", p=P)).then_inc(moe_w_in, 16)
                    else:
                        for dst, src in ((b1_sb, b1), (b2_sb, b2)):
                            sp.dma_start(dst[:, bass.ds(per * t, per), :],
                                         src[:, bass.ds(per * t, per), :]).then_inc(moe_w_in, 16)
            for q in range(FIRST_TAIL, NQ):
                window(q, q % AUG)

            def load_tile(n, j):
                sp.wait_ge(t1_done, n + 1)
                sp.dma_start(xg[j], xs_dram[bass.ts(n, P), :]).then_inc(xg_in[j], 16)

            sp.wait_ge(scattered, 16 * 4 * NT)
            for j in range(CH):
                load_tile(j, j)
            spread_sums(NQ - 1)
            for j in range(CH):
                load_tile(CH + j, j)
            store_inverses(NQ - 1)
            for j in range(CH):
                load_tile(2 * CH + j, j)
            load_inverses(NQ - 1)
            store_quad(NQ - 1)
            sp.wait_ge(s_done, NU * NQ + 1)

            def load_x_pair(m):
                sp.dma_start(x_all[:, bass.ts(m, 2), :], x_t[:, bass.ts(m, 2), :]).then_inc(x_all_in, 16)

            rounds = SLOTS // CH
            for m in range(NT // 2 - (rounds - 3)):
                load_x_pair(m)
            with sp.Fori(3, rounds) as t:
                for j in range(CH):
                    load_tile(CH * t + j, j)
                load_x_pair(t + NT // 2 - rounds)
            sp.wait_ge(a_stored, 16 * HQ * (NQ + 1))
            sp.dma_start(a_all[:, B - 1, :, :], a_f[:, B - 1, :, :]).then_inc(a_in, 16)

            def load_y(m, j):
                sp.dma_start(ya[j].rearrange("p t k d -> p t (k d)"), y_t[:, bass.ts(m, 2), :]).then_inc(ya_in[j], 16)

            for j in range(CH):
                sp.wait_ge(y_stored[j], 16 * (SLOTS // CH))
            for j in range(PAIRS):
                load_y(j, j)

            def pair_of_tiles(t, j, last):
                m = PAIRS * t + j
                if not last:
                    sp.wait_ge(gsum_done, m + 1)
                    load_y(m + PAIRS, j)
                sp.wait_ge(fin_done, m + 1 + DEEP)
                sp.dma_start(out_t[:, bass.ts(m, 2), :], x_all[:, bass.ts(m, 2), :]).then_inc(stored, 16)

            with sp.Fori(0, B - 1) as t:
                for j in range(PAIRS):
                    pair_of_tiles(t, j, False)
            for j in range(PAIRS):
                pair_of_tiles(B - 1, j, True)
            sp.wait_ge(stored, 16 * NT // 2)

        @block.gpsimd
        def _(pool):
            pool.sem_inc(o_normed, 1)
            pool.sem_inc(split_done, 8)
            pool.sem_inc(fin_done, DEEP)
            nc.gpsimd.memset(zeros[:, :], 0.0).then_inc(zeros_set, 1)
            for n in range(AUG):
                nc.gpsimd.memset(v_q[n][:, :, :, HD:2 * HD], 1.0).then_inc(ones_set, 1)

            def chunk(b, c):
                i = CHUNKS * b + c
                many = SLOTS // (B * CHUNKS)
                pool.dma_start(xs_t[:, bass.ts(i, many), :], many_zeros(many)).then_inc(xs_zero, 16)
                for n in range(4):
                    pool.wait_ge(split_step, 8 * i + 2 * n + 2)
                    nc.gpsimd.tensor_tensor(parts[c][n][:, 2, :], whole[c][n], parts[c][n][:, 1, :],
                                            ALU.subtract).then_inc(split_done, 1)

            pool.wait_ge(zeros_set, 1)
            pool.wait_ge(consts_in, 16 * NCONST)
            nc.gpsimd.tensor_copy(y_row[:, :, :], y_row_f.rearrange("p (t k) -> p t k", k=2)).then_inc(rows_ready, 1)
            with pool.Fori(0, B) as b:
                for c in range(CHUNKS):
                    chunk(b, c)

            def take_v(q, n):
                nc.gpsimd.tensor_copy(v_q[n][:, :, :, 0:HD],
                                      v_all[:, q, :, :].rearrange("p t (h d) -> p t h d", d=HD)
                                      ).then_inc(vq_ready, 1)

            def next_v(q, n):
                pool.wait_ge(pv_done, NTY * q + 3)
                take_v(q + 1, (n + 1) % AUG)

            pool.wait_ge(v_out, NT + 1)
            take_v(0, 0)

            step = [0]

            def after(ins):
                step[0] += 1
                ins.then_inc(route_step, 1)
                pool.wait_ge(route_step, step[0])

            def total(dst, src):
                n = src.shape[-1]
                while n > 2:
                    half = (n + 1) // 2
                    after(nc.gpsimd.tensor_tensor(src[:, :, 0:n - half], src[:, :, 0:n - half], src[:, :, half:n],
                                                  ALU.add))
                    n = half
                after(nc.gpsimd.tensor_tensor(dst, src[:, :, 0], src[:, :, 1], ALU.add))

            pool.wait_ge(counts_out, 1)
            after(nc.gpsimd.tensor_copy(gat[4], of_tile))
            src, dst, by = gat[4], upto_tile, 1
            while by < NT:
                nc.gpsimd.tensor_copy(dst[:, 0:by, :], src[:, 0:by, :])
                after(nc.gpsimd.tensor_tensor(dst[:, by:, :], src[:, by:, :], src[:, 0:NT - by, :], ALU.add))
                src, dst, by = dst, src, 2 * by
            assert src is upto_tile
            pool.sem_inc(summed, 1)
            pool.wait_ge(shares_ready, 1)
            for k, share in ((0, first), (1, low)):
                after(nc.gpsimd.tensor_tensor(gat[0], gat[1 + 2 * k], over(alpha_sb[:, :], NT), ALU.mult))
                total(where, gat[0])
                after(nc.gpsimd.tensor_tensor(weight[:, :, k], where, share, ALU.mult))
            after(nc.gpsimd.tensor_tensor(dst, src, of_tile, ALU.subtract))
            after(nc.gpsimd.tensor_tensor(dst, dst, ahead_in, ALU.add))
            pool.wait_ge(bases_ready, 1)
            after(nc.gpsimd.tensor_tensor(dst, dst, over(base, NT), ALU.add))
            for k in range(2):
                after(nc.gpsimd.tensor_tensor(gat[0], gat[1 + 2 * k], dst, ALU.mult))
                total(slot_f[:, :, k], gat[0])
            after(nc.gpsimd.tensor_copy(slot[:, :, :], slot_f))
            pool.sem_inc(routed, 1)
            next_v(0, 0)

            def normalise(q):
                pool.wait_ge(inverse_in, 16 * HQ * q + 16 * HQ)
                pool.wait_ge(a_stored, 16 * HQ * q + 16 * HQ)
                nc.gpsimd.tensor_tensor(o_norm, oT, inverse, ALU.mult).then_inc(o_normed, 1)

            nc.gpsimd.memset(inverse, 1.0).then_inc(sums_set, 1)
            for c in range(CHUNKS):
                pool.wait_ge(xn_out[c], 16 * (B + 1))
            pool.wait_ge(xs_zero, 16 * B * CHUNKS)
            pool.wait_ge(table_out, 16)
            pool.wait_ge(rows_ready, 1)
            with pool.Fori(0, ROUNDS) as t:
                for r in range(AUG):
                    q = AUG * t + r + 1
                    next_v(q, (r + 1) % AUG)
                    normalise(q - 1)
                    if r < 2:
                        i = 2 * t + r
                        now = bass.ts(i, ST)
                        pool.dma_start(x_move[:, :, :], xn_t[:, now, :]).then_inc(x_moved, 16)
                        nc.gpsimd.tensor_copy(slot_now[:, :, :], slot[:, now, :])
                        nc.gpsimd.tensor_copy(y_row_now[:, :, :], y_row[:, now, :]).then_inc(rows_ready, 1)
                        pool.wait_ge(rows_ready, i + 2)
                        pool.wait_ge(x_moved, 16 * i + 16)
                        pool.sem_inc(passed, 1)
                        for s in range(ST):
                            for k in range(2):
                                nc.gpsimd.indirect_dma_start(
                                    out=xs_dram, in_=x_move[:, s, :], in_offset=None,
                                    out_offset=bass.IndirectOffsetOnAxis(ap=slot_now[:, s, k:k + 1], axis=0)
                                    ).then_inc(scattered, 16)
                                nc.gpsimd.indirect_dma_start(
                                    out=slot_dram, in_=y_row_now[:, s, k:k + 1], in_offset=None,
                                    out_offset=bass.IndirectOffsetOnAxis(ap=slot_now[:, s, k:k + 1], axis=0)
                                    ).then_inc(scattered, 16)
                        pool.wait_ge(scattered, 16 * 4 * ST * i + 16 * 4 * ST)
                        pool.sem_inc(passed, 1)
            pool.dma_start(y_row_of[:, :], slot_dram.rearrange("(n p) o -> p (n o)", p=P),
                           allow_slow_non_contiguous=True).then_inc(table_in, 16)
            for q in range(FIRST_TAIL, NQ):
                if q < NQ - 1:
                    next_v(q, q % AUG)
                normalise(q - 1)
            pool.wait_ge(table_in, 16)

            def scatter_outputs(t, first):
                for j in range(CH):
                    if not first:
                        pool.wait_ge(y_stored[j], 16 * t)
                    nc.gpsimd.tensor_copy(y_rows[:, j:j + 1], y_row_of[:, bass.ds(CH * t + j, 1)]).then_inc(y_rows_ready, 1)
                    pool.wait_ge(y_rows_ready, CH * t + j + 1)
                    pool.sem_inc(passed, 1)
                    pool.wait_ge(y_out, CH * t + j + 3)
                    pool.sem_inc(passed, 1)
                    nc.gpsimd.indirect_dma_start(
                        out=y_dram, in_=ysb[j], in_offset=None,
                        out_offset=bass.IndirectOffsetOnAxis(ap=y_rows[:, j:j + 1], axis=0)).then_inc(y_stored[j], 16)

            scatter_outputs(0, True)
            normalise(NQ - 1)
            with pool.Fori(1, SLOTS // CH) as t:
                scatter_outputs(t, False)

            pool.wait_ge(x_all_in, 16 * NT // 2)
            with pool.Fori(0, B) as t:
                for j in range(PAIRS):
                    m = PAIRS * t + j
                    pool.wait_ge(sg_done, m + 1 + DEEP)
                    pool.sem_inc(passed, 1)
                    tokens = x_all[:, bass.ts(m, 2), :]
                    nc.gpsimd.tensor_tensor(tokens, tokens, so[j].rearrange("p (t d) -> p t d", d=D),
                                            ALU.add).then_inc(fin_done, 1)

        @block.scalar
        def _(act):
            act.sem_inc(proj_out, 2)
            act.sem_inc(exp_done, 2)
            act.sem_inc(o_out, 1)
            act.sem_inc(xgT_out, 2)

            def roots(i):
                act.wait_ge(var_ready, i + 1)
                nc.scalar.activation(std[:, :], veps[:, :], ACT.Sqrt).then_inc(std_ready, 1)

            def take_transposed(i, c, k):
                act.wait_ge(xpose_done, 2 * i + k + 3)
                nc.scalar.activation(xnT[c][:, k, :], bank(6), ACT.Copy).then_inc(xT_ready, 1)

            def chunk(b, c, more=B * CHUNKS):
                i = CHUNKS * b + c
                act.wait_ge(parts_out[c], 64 * b + 64)
                for n, (side, m) in enumerate(SIDES):
                    act.wait_ge(proj_done, 4 * i + n + 1)
                    act.wait_ge(split_done, 4 * i + n + 1)
                    bias = (kbs_sb, qb_sb)[side][:, m:m + 1]
                    scale = (SCALE, 1.0)[side]
                    nc.scalar.activation(whole[c][n], bank(4 + n % 2), ACT.Identity, bias=bias, scale=scale)
                    nc.scalar.activation(parts[c][n][:, 0, :], bank(4 + n % 2), ACT.Identity, bias=bias,
                                         scale=scale).then_inc(proj_out, 1)
                    if n == 2 and more > 0:
                        for k in range(KT):
                            take_transposed(i + 1, 1 - c, k)
                        if more > 1:
                            roots(i + 2)

            for i in range(CHUNKS):
                roots(i)
            for k in range(KT):
                take_transposed(0, 0, k)
            act.wait_ge(weights_in, 16 * len(WEIGHTS))
            act.wait_ge(bias_ready, 1)
            with act.Fori(0, B - 1) as b:
                for c in range(CHUNKS):
                    chunk(b, c)
            for c in range(CHUNKS):
                chunk(B - 1, c, CHUNKS - c - 1)
            act.wait_ge(parts_out[0], 16 * 4 * (B + 1))

            def evacuate(q):
                act.wait_ge(routed, 1)
                act.wait_ge(o_normed, q + 1)
                act.wait_ge(pv_done, NTY * q + NTY + 3)
                nc.scalar.activation(oT, bank(6, 2), ACT.Copy).then_inc(o_out, 1)

            def window(q, first=False):
                for i in range(NU):
                    k, u, unit = UNITS[i // 2]
                    half = slice(i % 2 * BANK, (i % 2 + 1) * BANK)
                    if first and k == 1 and u == 0 and i % 2 == 0:
                        act.wait_ge(parts_out[1], 16 * 4 * (B + 1))
                    if k == 0 and i == 0:
                        act.wait_ge(pv_done, NTY * q + 1)
                    elif k == 0 and SLOT[k, u] == 0 and i % 2 == 0:
                        act.wait_ge(pv_done, NTY * q + 3)
                    elif k > 1 and u == 0 and i % 2 == 0:
                        act.wait_ge(pv_done, NTY * q + k + 2)
                    act.wait_ge(s_done, NU * q + i + 2)
                    nc.scalar.activation(probs[SLOT[k, u]][:, half], score_bank(q, i), ACT.Exp).then_inc(exp_done, 1)
                    if i == EVACUATE and not first:
                        evacuate(q - 1)
                    if i == COUNT_STEP and first:
                        act.wait_ge(gap_ready, 1)
                        nc.scalar.activation(gexp, gap, ACT.Exp).then_inc(gexp_ready, 1)
                        act.wait_ge(counted, 1)
                        for n, dst in enumerate((ahead_in, of_tile)):
                            ins = nc.scalar.activation(dst.rearrange("p t e -> p (t e)"),
                                                       bank(6 + n)[:, 0:NT * E], ACT.Copy)
                        ins.then_inc(counts_out, 1)

            window(0, first=True)
            with act.Fori(0, ROUNDS) as t:
                for r in range(AUG):
                    window(AUG * t + r + 1)
            for q in range(FIRST_TAIL, NQ - 1):
                window(q)
            act.wait_ge(vq_ready, NQ)
            act.wait_ge(a_stored, 16 * HQ * (HQ * (B - 1) + 1))
            for b in range(B - 1):
                act.dma_start(a_all[:, b, :, :], a_f[:, b, :, :]).then_inc(a_in, 16)
            window(NQ - 1)
            evacuate(NQ - 1)

            def x_evacuate(n, j):
                act.wait_ge(t1_done, n + 1 + CH)
                nc.scalar.activation(xgT[j % CH], bank(j % 2)[:, 0:D], ACT.Copy).then_inc(xgT_out, 1)

            def gelu(n, j):
                act.wait_ge(h_out, n + 3)
                nc.scalar.activation(hid[j % CH], hid[j % CH], ACT.Gelu).then_inc(g_done, 1)

            def take_weights(n, j):
                e = act.value_load(tile_expert[0:1, bass.ds(n, 1)], min_val=0, max_val=E - 1)
                if not isinstance(n, int) or n >= 2:
                    act.wait_ge(l1_done, n - 1)
                    act.sem_inc(passed, 1)
                nc.scalar.activation(w1_now[j % 2], w1_sb[:, bass.ds(e * KT, KT), :], ACT.Copy).then_inc(w1_ready, 1)

            act.wait_ge(piece_used, LAST_ITEM + 2)
            act.wait_ge(moe_w_in, 16 * 2 * AUG * ROUNDS)
            skewed(act, ((x_evacuate, 3), (gelu, 2), (take_weights, 4)))

            act.wait_ge(a_in, 16 * B)

            nc.scalar.activation(std[:, :], veps[:, :], ACT.Silu)

            def take_a(t, j):
                nc.scalar.activation(aT[j], a_all[:, t, :, 2 * P * j:2 * P * (j + 1)], ACT.Identity).then_inc(aT_ready, 1)

            def scale_first(t, j):
                m = PAIRS * t + j
                act.wait_ge(ya_in[j], 16 * t + 16)
                act.wait_ge(sg_done, m + 1)
                act.sem_inc(passed, 1)
                for i in range(2):
                    ins = nc.scalar.activation(gsum[j][:, i * D:(i + 1) * D], ya[j][:, i, 0, :], ACT.Identity,
                                               scale=weight[:, bass.ds(2 * m + i, 1), 0])
                ins.then_inc(y_scaled, 1)

            def silu(t, j):
                act.wait_ge(gsum_done, PAIRS * t + j + 1)
                nc.scalar.activation(gsum[j], gsum[j], ACT.Silu).then_inc(silu_done, 1)
                if not isinstance(t, int) or t < B - 1:
                    act.wait_ge(s_proj, PAIRS * t + j + 1)
                    act.sem_inc(passed, 1)
                    take_a(t + 1, j)

            for j in range(PAIRS):
                take_a(0, j)

            in_turn(act, scale_first, silu)

        @block.vector
        def _(dve):
            dve.sem_inc(v_out, 1)
            dve.sem_inc(piece_used, 2)
            dve.sem_inc(h_out, 2)
            dve.sem_inc(y_out, 2)
            dve.sem_inc(s_used, DEEP)
            dve.sem_inc(sg_done, DEEP)

            def statistics(i, b, c):
                dve.wait_ge(x_in[c], 16 * b + 16)
                if not isinstance(i, int) or i >= CHUNKS:
                    dve.wait_ge(xn_ready, i - 1)
                for t in range(CT):
                    ins = nc.vector.bn_stats(stats[:, c, t, :], xb[c][:, t, :])
                ins.then_inc(ln_step, 1)
                dve.wait_ge(ln_step, 2 * i + 1)
                dve.sem_inc(passed, 1)
                for t in range(CT):
                    ins = nc.vector.bn_aggr(mv[:, c, t, :], stats[:, c, t, :])
                ins.then_inc(ln_step, 1)
                dve.wait_ge(ln_step, 2 * i + 2)
                nc.vector.tensor_scalar(veps[:, :], mv[:, c, :, 1], EPS, None, ALU.add).then_inc(var_ready, 1)

            def inverse_roots(i, c):
                dve.wait_ge(std_ready, i + 1)
                nc.vector.reciprocal(rstd[:, c, :], std[:, :]).then_inc(rstd_ready, 1)

            def normalise(i, b, c):
                dve.wait_ge(rstd_ready, i + 1)
                if not isinstance(i, int) or i > 0:
                    dve.wait_ge(xpose_done, 2 * i)
                dve.wait_ge(xn_out[c], 16 * b + 16)
                dve.sem_inc(passed, 1)
                for t in range(CT):
                    ins = nc.vector.tensor_scalar(xnb[c][:, t, :], xb[c][:, t, :], mv[:, c, t, 0:1],
                                                  rstd[:, c, t:t + 1], ALU.subtract, ALU.mult)
                ins.then_inc(xn_ready, 1)

            def split(i, c, n):
                dve.wait_ge(proj_out, 4 * i + n + 3)
                nc.vector.tensor_tensor(whole[c][n], whole[c][n], parts[c][n][:, 0, :],
                                        ALU.subtract).then_inc(split_step, 1)
                dve.wait_ge(split_step, 8 * i + 2 * n + 1)
                nc.vector.tensor_copy(parts[c][n][:, 1, :], whole[c][n]).then_inc(split_step, 1)

            def take_values(i, b, c, t):
                dve.wait_ge(v_done, 4 * i + t + 1)
                at_ = CT * c + t
                nc.vector.tensor_tensor(v_all[:, bass.ts(b, HQ), at_, :],
                                        bank(7)[:, 0:D].rearrange("p (g f) -> p g f", f=QF),
                                        vb_sb[:, :].rearrange("p (g f) -> p g f", f=QF), ALU.add)
                nc.vector.tensor_copy(logits[:, TB * b + at_, :], bank(7)[:, D:D + E]).then_inc(v_out, 1)

            def chunk(b, c, more=B * CHUNKS, item=lambda n: None):
                i = CHUNKS * b + c
                for n in range(4):
                    split(i, c, n)
                    item(2 * n)
                    take_values(i, b, c, n)
                    item(2 * n + 1)
                    if n == 0 and more > 0:
                        normalise(i + 1, b + c, 1 - c)
                    if n == 1 and more > 1:
                        statistics(i + 2, b + 1, c)
                    if n == 3 and more > 1:
                        inverse_roots(i + 2, c)

            mparts = [msplit[:, s * TB * HQ:(s + 1) * TB * HQ].rearrange("p (h t) -> p h t", t=TB)
                      for s in range(NSPLIT)]

            def reduce_piece(s, banks, piece):
                dve.wait_ge(piece_done, s + 1)
                ib, h, heads, pitch = PIECES[piece]
                src = banks[:, 0:heads * pitch].rearrange("p (h j) -> p h j", h=heads)[:, :, 0:P * (ib + 1)]
                nc.vector.tensor_reduce(mxa[:, h:h + heads, ib], src, AX.X, ALU.max).then_inc(piece_used, 1)

            def split_maxima(q, s):
                dve.wait_ge(piece_used, s + 3)
                nc.vector.tensor_copy(mparts[0], mxa[:, :, :]).then_inc(m_step, 1)
                dve.wait_ge(m_step, 3 * q + 1)
                nc.vector.tensor_tensor(mrest[:, :, :], mxa[:, :, :], mparts[0], ALU.subtract).then_inc(m_step, 1)
                dve.wait_ge(m_step, 3 * q + 2)
                nc.vector.tensor_copy(mparts[1], mrest[:, :, :]).then_inc(m_step, 1)
                dve.wait_ge(m_step, 3 * q + 3)
                nc.vector.tensor_tensor(mparts[2], mrest[:, :, :], mparts[1], ALU.subtract).then_inc(m_split, 1)

            def take_maxima(q, s, banks):
                dve.wait_ge(piece_done, s + 1)
                if not isinstance(q, int) or q > 0:
                    dve.wait_ge(m_in, 48 * q)
                nc.vector.tensor_copy(mT[:, :], banks.bitcast(bf16)[0:NSPLIT * TB * HQ, 0:P]).then_inc(mT_ready, 1)
                dve.wait_ge(mT_ready, q + 1)
                dve.sem_inc(piece_used, 1)

            def invert_sums(q):
                dve.wait_ge(sums_in, 16 * HQ * q + 16 * HQ)
                nc.vector.reciprocal(sums[:, :], sums[:, :]).then_inc(inverse_ready, 1)

            def follow_item(q, base, i, item):
                what, d, piece = item
                s, banks = base + i, pair(base, i)
                if what == "maxima":
                    take_maxima(q + d, s, banks)
                else:
                    if piece == 0 and i > 0:
                        dve.wait_ge(m_split, q + d)
                    reduce_piece(s, banks, piece)
                    if piece == NP - 1:
                        split_maxima(q + d, s)

            for c in range(CHUNKS):
                statistics(c, 0, c)
                inverse_roots(c, c)
                if c == 0:
                    normalise(0, 0, 0)
            dve.wait_ge(weights_in, 16 * len(WEIGHTS))
            nc.vector.tensor_scalar(kbs_sb[:, :], kb_sb[:, :], SCALE, None, ALU.mult).then_inc(bias_ready, 1)
            with dve.Fori(0, PLAIN) as b:
                for c in range(CHUNKS):
                    chunk(b, c)
            ahead_of_windows = iter(list(enumerate(stream(0))))

            def next_items(i):
                def after_step(n):
                    for _ in range(items_at(i, n)):
                        s, item = next(ahead_of_windows)
                        follow_item(0, 0, s, item)

                return after_step

            for b in range(PLAIN, B):
                for c in range(CHUNKS):
                    chunk(b, c, (B - b) * CHUNKS - c - 1, next_items(CHUNKS * (b - PLAIN) + c))
            dve.wait_ge(consts_in, 16 * NCONST)

            step = [0]

            def after(ins):
                step[0] += 1
                ins.then_inc(gate_step, 1)
                dve.wait_ge(gate_step, step[0])

            dve.wait_ge(v_out, NT + 1)
            for c in range(CHUNKS):
                dve.wait_ge(xn_out[c], 16 * (B + 1))
            index = over(e_index, NT)


            def choose(values, top, chosen):
                after(nc.vector.tensor_reduce(top, values, AX.X, ALU.max))
                after(nc.vector.tensor_tensor(gat[0], values, spread(top, E), ALU.is_lt))
                after(nc.vector.scalar_tensor_tensor(gat[0], gat[0], float(E), index, ALU.mult, ALU.add))
                after(nc.vector.tensor_reduce(where, gat[0], AX.X, ALU.min))
                after(nc.vector.tensor_tensor(chosen, index, spread(where, E), ALU.is_equal))

            choose(logits[:, :, :], best, gat[1])
            after(nc.vector.scalar_tensor_tensor(gat[2], gat[1], NEG, logits[:, :, :], ALU.mult, ALU.add))
            choose(gat[2], second, gat[3])
            nc.vector.tensor_tensor(gap, second, best, ALU.subtract).then_inc(gap_ready, 1)
            after(nc.vector.tensor_tensor(picked_b[:, :, :], gat[1], gat[3], ALU.add))
            dve.sem_inc(picked, 1)
            def place_experts():
                dve.wait_ge(gexp_ready, 1)
                after(nc.vector.tensor_scalar(norm, gexp, 1.0, None, ALU.add))
                after(nc.vector.reciprocal(first, norm))
                after(nc.vector.tensor_tensor(low, gexp, first, ALU.mult))
                dve.sem_inc(shares_ready, 1)
                dve.wait_ge(summed, 1)
                after(nc.vector.tensor_tensor(need, spread(upto_tile[:, NT - 1, :], NT), over(multiples, E), ALU.is_gt))
                after(nc.vector.tensor_reduce(tiles, need, AX.X, ALU.add))
                after(nc.vector.tensor_tensor(ahead, over(tiles, E), is_ahead, ALU.mult))
                after(nc.vector.tensor_reduce(base, ahead, AX.X, ALU.add))
                after(nc.vector.tensor_tensor(upto, base, tiles, ALU.add))
                after(nc.vector.tensor_scalar(base, base, float(P), None, ALU.mult))
                after(nc.vector.tensor_tensor(full, spread(tile_index, E - 1), over(upto[:, 0:E - 1], SLOTS),
                                              ALU.is_ge))
                after(nc.vector.tensor_reduce(expert_f, full, AX.X, ALU.add))
                after(nc.vector.tensor_copy(tile_expert[:, :], expert_f))
                dve.sem_inc(bases_ready, 1)

            def follow(q, base, items, first=False):
                for i, item in enumerate(items):
                    if i == EXPERTS_ITEM and first:
                        place_experts()
                    if i == INVERT_ITEM and not first:
                        invert_sums(q - 1)
                    follow_item(q, base, i, item)

            follow(0, PRO, stream(1), first=True)
            with dve.Fori(0, ROUNDS) as t:
                for r in range(AUG):
                    q = AUG * t + r + 1
                    follow(q, PRO + WIN * q, stream(1))
            for q in range(FIRST_TAIL, NQ - 1):
                follow(q, PRO + WIN * q, stream(1, more=NQ - 1 - q))
            invert_sums(NQ - 2)

            def h_evacuate(n, j):
                e = dve.value_load(tile_expert[0:1, bass.ds(n, 1)], min_val=0, max_val=E - 1)
                dve.wait_ge(l1_done, n + 1)
                nc.vector.tensor_tensor(hid[j % CH], bank(2 + j % 2)[:, 0:D], b1_sb[:, e, :], ALU.add).then_inc(h_out, 1)

            def y_evacuate(n, j):
                if isinstance(n, int) and n == 0:
                    invert_sums(NQ - 1)
                e = dve.value_load(tile_expert[0:1, bass.ds(n, 1)], min_val=0, max_val=E - 1)
                dve.wait_ge(l2_done, n + 1)
                if not isinstance(n, int) or n >= CH:
                    dve.wait_ge(y_stored[j % CH], 16 * rnd_of(n, j))
                nc.vector.tensor_tensor(ysb[j % CH], bank(6 + j % 2)[:, 0:D], b2_sb[:, e, :], ALU.add).then_inc(y_out, 1)

            dve.wait_ge(pv_done, NTY * NQ + 3)
            dve.wait_ge(moe_w_in, 16 * 2 * AUG * ROUNDS)
            dve.wait_ge(routed, 1)
            skewed(dve, ((h_evacuate, 2), (y_evacuate, 0)))

            def add_second(t, j):
                m = PAIRS * t + j
                dve.wait_ge(y_scaled, m + 1)
                for i in range(2):
                    part = gsum[j][:, i * D:(i + 1) * D]
                    ins = nc.vector.scalar_tensor_tensor(part, ya[j][:, i, 1, :], weight[:, bass.ds(2 * m + i, 1), 1],
                                                         part, ALU.mult, ALU.add)
                ins.then_inc(gsum_done, 1)

            def product(t, j):
                m = PAIRS * t + j
                dve.wait_ge(s_proj, m + 1)
                dve.wait_ge(fin_done, m + 1)
                nc.vector.tensor_tensor(so[j].rearrange("p (t d) -> p t d", d=D),
                                        bank(j).rearrange("p (t d) -> p t d", d=D), over(ob_sb[:, :], 2),
                                        ALU.add).then_inc(s_used, 1)
                dve.wait_ge(s_used, m + 1 + DEEP)
                dve.wait_ge(silu_done, m + 1)
                nc.vector.tensor_tensor(so[j], so[j], gsum[j], ALU.mult).then_inc(sg_done, 1)

            in_turn(dve, add_second, product)

        @block.tensor
        def _(pe):
            pe.sem_inc(xpose_done, 2)
            pe.sem_inc(s_done, 1)
            pe.sem_inc(pv_done, 3)
            pe.sem_inc(t1_done, CH)

            def transposes(i, c, k):
                if not isinstance(i, int) or i > 0 or k > 0:
                    pe.wait_ge(xT_ready, 2 * i + k)
                pe.wait_ge(xn_ready, i + 1)
                for t in range(CT):
                    ins = nc.tensor.transpose(bank(6)[:, t * P:(t + 1) * P], xnb[c][:, t, k * P:(k + 1) * P], idf[:, :])
                ins.then_inc(xpose_done, 1)

            def project(i, c, n):
                side, m = SIDES[n]
                pe.wait_ge(xT_ready, 2 * i + 2)
                pe.wait_ge(proj_out, 4 * i + n + 1)
                for k in range(KT):
                    ins = nc.tensor.matmul(bank(4 + n % 2), (wk_sb, wq_sb)[side][:, k, m * P:(m + 1) * P],
                                           xnT[c][:, k, :], start=(k == 0), stop=(k == KT - 1))
                ins.then_inc(proj_done, 1)

            def values(i, c, t):
                pe.wait_ge(v_out, 4 * i + t + 1)
                for k in range(KT):
                    ins = nc.tensor.matmul(bank(7)[:, 0:D + E], xnT[c][:, k, t * P:(t + 1) * P], wvg_sb[:, k, :],
                                           start=(k == 0), stop=(k == KT - 1))
                ins.then_inc(v_done, 1)

            def chunk(b, c, more=B * CHUNKS, item=lambda n: None):
                i = CHUNKS * b + c
                for n in range(4):
                    project(i, c, n)
                    item(2 * n)
                    if n == 2 and more > 0:
                        transposes(i + 1, 1 - c, 0)
                    values(i, c, n)
                    item(2 * n + 1)
                    if n == 2 and more > 0:
                        transposes(i + 1, 1 - c, 1)

            pe.wait_ge(ident_in, 16)
            for k in range(KT):
                transposes(0, 0, k)
            pe.wait_ge(weights_in, 16 * len(WEIGHTS))
            with pe.Fori(0, PLAIN) as b:
                for c in range(CHUNKS):
                    chunk(b, c)

            def send_piece(n, s, banks, piece):
                ib, h0, heads, pitch = PIECES[piece]
                width = P * (ib + 1)
                pe.wait_ge(piece_used, s + 1)
                for h in range(heads):
                    for lo in range(0, width, BANK):
                        hi = min(lo + BANK, width)
                        out_ = banks[:, h * pitch + lo:h * pitch + hi]
                        ins = nc.tensor.matmul(out_, k_aug[n][0:SCORE_ROWS, h0 + h, ib * P:(ib + 1) * P],
                                               q_aug[n][0:SCORE_ROWS, h0 + h, lo:hi], start=True, stop=hi < width)
                        if hi == width:
                            ins = nc.tensor.matmul(out_[:, hi - lo - P:], idb[:, :], mask_sb[:, :],
                                                   start=False, stop=True)
                ins.then_inc(piece_done, 1)

            def send_maxima(q, s, banks):
                pe.wait_ge(m_split, q + 1)
                pe.wait_ge(piece_used, s + 1)
                nc.tensor.transpose(banks.bitcast(bf16)[0:NSPLIT * TB * HQ, 0:P], msplit[:, :],
                                    idb[:, :]).then_inc(piece_done, 1)

            def send(q, n, s, banks, item):
                what, d, piece = item
                if what == "maxima":
                    send_maxima(q + d, s, banks)
                else:
                    if piece == 0:
                        pe.wait_ge(aug_in[(n + d) % AUG], 192 * filled(q + d) + 192)
                    send_piece((n + d) % AUG, s, banks, piece)

            def half_unit(q, n, i):
                k, u, unit = UNITS[i // 2]
                first, end = i % 2 * BANK, (i % 2 + 1) * BANK
                if not is_last(q):
                    pe.wait_ge(exp_done, NU * q + i + 1)
                elif i >= 4:
                    pe.wait_ge(exp_done, NU * q + i - 3)
                elif i == 0:
                    pe.wait_ge(piece_used, LAST_ITEM + 2)
                for jb, h, col0 in unit:
                    lo, hi = max(first, col0), min(end, col0 + T - P * jb)
                    if lo >= hi:
                        continue
                    out_ = score_bank(q, i)[:, lo - first:hi - first]
                    i0 = P * jb + lo - col0
                    ins = nc.tensor.matmul(out_, q_aug[n][0:ALL_ROWS, h, jb * P:(jb + 1) * P],
                                           k_aug[n][0:ALL_ROWS, h, i0:i0 + hi - lo], start=True, stop=lo > col0)
                    if lo == col0:
                        ins = nc.tensor.matmul(out_[:, 0:P], idb[:, :], maskT_sb[:, :], start=False, stop=True)
                ins.then_inc(s_done, 1)

            def group_outputs(n, k, jb, c):
                lo, hi = max(P * jb, c * BANK), (c + 1) * BANK
                last = jb == (TB // 2 - 1 if c == 0 else TB // 2)
                for u, unit in enumerate(TYPES[k]):
                    for part, h, col0 in unit:
                        if part == jb:
                            at_ = col0 + lo - P * jb
                            ins = nc.tensor.matmul(ps[2 * HD * h:2 * HD * (h + 1), 6 * BANK + lo:6 * BANK + hi],
                                                   v_q[n][:, jb, h, :], probs[SLOT[k, u]][:, at_:at_ + hi - lo],
                                                   start=(jb == 0), stop=last)
                return ins

            def send_group(q, n, g):
                k, jb, c = GROUPS[g]
                if g == 0:
                    pe.wait_ge(vq_ready, q + 1)
                    pe.wait_ge(o_out, q + 1)
                    pe.wait_ge(counts_out, 1)
                if g == 0 or GROUPS[g - 1][0] != k:
                    pe.wait_ge(exp_done, NU * q + LAST_OF_TYPE[k] + 2)
                ins = group_outputs(n, k, jb, c)
                if g + 1 == len(GROUPS) or GROUPS[g + 1][0] != k:
                    ins.then_inc(pv_done, 1)

            in_loop = [None]

            def filled(q):
                if isinstance(q, int):
                    return q // AUG
                return in_loop[0] + 1

            def window(q, n, base, items, first=False):
                sent = 0
                pe.wait_ge(m_in, 48 * q + 48)
                for i in range(NU):
                    half_unit(q, n, i)
                    if i == COUNT_STEP and first:
                        pe.wait_ge(picked, 1)
                        for h in range(2):
                            ins = nc.tensor.matmul(bank(6 + h)[:, 0:NT * E], before_sb[:, h * P:(h + 1) * P],
                                                   picked_b[:, :, :].rearrange("p t e -> p (t e)"),
                                                   start=True, stop=True)
                        ins.then_inc(counted, 1)
                    if i in GROUP_STEP:
                        send_group(q, n, GROUP_STEP.index(i))
                    elif NU + i in GROUP_STEP:
                        if not first:
                            send_group(q - 1, (n - 1) % AUG, GROUP_STEP.index(NU + i))
                    elif sent < len(items):
                        send(q, n, base + sent, pair(base, sent), items[sent])
                        sent += 1

            pe.wait_ge(consts_in, 16 * NCONST)
            ahead_of_windows = iter(list(enumerate(stream(0))))

            def next_items(i):
                def after_step(n):
                    for _ in range(items_at(i, n)):
                        s, item = next(ahead_of_windows)
                        send(0, 0, s, pair(s, 0), item)

                return after_step

            for b in range(PLAIN, B):
                for c in range(CHUNKS):
                    chunk(b, c, (B - b) * CHUNKS - c - 1, next_items(CHUNKS * (b - PLAIN) + c))
            pe.wait_ge(ones_set, AUG)
            window(0, 0, PRO, stream(1), first=True)
            with pe.Fori(0, ROUNDS) as t:
                in_loop[0] = t
                for r in range(AUG):
                    q = AUG * t + r + 1
                    window(q, (r + 1) % AUG, PRO + WIN * q, stream(1))
            for q in range(FIRST_TAIL, NQ):
                window(q, q % AUG, PRO + WIN * q, stream(1, more=NQ - 1 - q))
            for g, step in enumerate(GROUP_STEP):
                if step >= NU:
                    send_group(NQ - 1, (NQ - 1) % AUG, g)
            pe.wait_ge(piece_used, LAST_ITEM + 2)
            pe.wait_ge(moe_w_in, 16 * 2 * AUG * ROUNDS)
            pe.wait_ge(routed, 1)

            def x_transpose(n, j):
                pe.wait_ge(xg_in[j % CH], 16 * rnd_of(n, j) + 16)
                for k in range(KT):
                    ins = nc.tensor.transpose(bank(j % 2)[:, k * P:(k + 1) * P], xg[j % CH][:, k * P:(k + 1) * P],
                                              idf[:, :])
                ins.then_inc(t1_done, 1)

            chosen = {}

            def second_expert(n, j):
                chosen[2] = pe.value_load(tile_expert[0:1, bass.ds(n, 1)], min_val=0, max_val=E - 1)

            def hidden(n, j):
                pe.wait_ge(xgT_out, n + 3)
                pe.wait_ge(w1_ready, n + 1)
                pe.wait_ge(h_out, n + 1)
                for m in range(KT):
                    for k in range(KT):
                        ins = nc.tensor.matmul(bank(2 + j % 2)[:, m * P:(m + 1) * P],
                                               w1_now[j % 2][:, k, m * P:(m + 1) * P], xgT[j % CH][:, k * P:(k + 1) * P],
                                               start=(k == 0), stop=(k == KT - 1))
                ins.then_inc(l1_done, 1)

            def expert_out(n, j):
                e = chosen[2]
                if isinstance(n, int) and n == 0:
                    pe.wait_ge(o_out, NQ + 1)
                pe.wait_ge(g_done, n + 1)
                pe.wait_ge(y_out, n + 1)
                for k in range(KT):
                    ins = nc.tensor.matmul(bank(6 + j % 2)[:, 0:D], hid[j % CH][:, k * P:(k + 1) * P],
                                           w2_sb[:, e * KT + k, :], start=(k == 0), stop=(k == KT - 1))
                ins.then_inc(l2_done, 1)

            skewed(pe, ((x_transpose, 3), (hidden, 2), (second_expert, 0), (expert_out, 0)))

            pe.wait_ge(y_out, SLOTS + 2)
            with pe.Fori(0, B) as t:
                for j in range(PAIRS):
                    pe.wait_ge(aT_ready, PAIRS * t + j + 1)
                    pe.wait_ge(s_used, PAIRS * t + j + 1)
                    for i in range(2):
                        for k in range(KT):
                            ins = nc.tensor.matmul(bank(j)[:, i * D:(i + 1) * D], aT[j][:, k, i * P:(i + 1) * P],
                                                   wo_sb[:, k, :], start=(k == 0), stop=(k == KT - 1))
                    ins.then_inc(s_proj, 1)


def kernel(**inputs):
    import numpy as np
    import concourse.bacc as bacc
    from concourse.bass_utils import run_bass_kernel_spmd

    def rows(n, m):
        return np.ascontiguousarray(np.broadcast_to(n, (m,) + n.shape))

    def block_(name):
        return np.asarray(inputs[name])

    bf = mybir.dt.np(bf16)
    pos = np.arange(T)
    tile, within = pos // P, pos % P
    border = np.arange(1, TB)[:, None]
    k_rows = np.concatenate([(tile[None] >= border).astype(np.float32), -within[None], np.ones((1, T))])
    q_rows = np.concatenate([-P * (tile[None] < border).astype(np.float32), np.ones((1, T)), within[None],
                             -np.ones((NSPLIT, T))])
    heads = lambda a: np.ascontiguousarray(np.broadcast_to(a[:, None, :], (a.shape[0], HQ, T))).astype(bf)
    low = np.tril(np.ones((P, P), bool))
    ahead = np.tril(np.ones((E, E)), -1).reshape(-1)
    shape_numbers = np.concatenate([np.arange(E), P * np.arange(NT), ahead, np.arange(SLOTS)])
    row = np.arange(P)[:, None]
    y_rows = 2 * (P * np.repeat(np.arange(NT), 2)[None] + row) + np.tile(np.arange(2), NT)[None]
    numbers = np.concatenate([rows(shape_numbers, P), y_rows], axis=1)
    args = {
        "x": block_("L0_attn_x"),
        "wqT": block_("L0_attn_q_w").T,
        "wkT": block_("L0_attn_k_w").T,
        "wvT": block_("L0_attn_v_w").T,
        "woT": block_("L0_attn_o_w").T,
        "qb": block_("L0_attn_q_b").reshape(KT, P).T,
        "kb": block_("L0_attn_k_b").reshape(KT, P).T,
        "vb": rows(block_("L0_attn_v_b"), P),
        "ob": rows(block_("L0_attn_o_b"), P),
        "gate": block_("L0_ffn_gate_w"),
        "w1": block_("L0_ffn_fc1_w"),
        "b1": np.broadcast_to(block_("L0_ffn_fc1_b").reshape(E, KT, P).transpose(2, 0, 1)[..., None],
                              (P, E, KT, P)).reshape(P, E, D),
        "w2": block_("L0_ffn_fc2_w"),
        "b2": rows(block_("L0_ffn_fc2_b"), P),
        "alpha": rows(block_("L0_ffn_alpha"), P),
        "ident_f": np.eye(P, dtype=np.float32),
        "ident_b": np.eye(P).astype(bf),
        "mask_neg": np.where(low, 0.0, NEG).astype(bf),
        "mask_negT": np.where(low.T, 0.0, NEG).astype(bf),
        "before": np.concatenate([np.triu(np.ones((P, P)), 1), np.ones((P, P))], axis=1).astype(bf),
        "k_rows": heads(k_rows),
        "q_rows": heads(q_rows),
        "numbers": numbers.astype(np.float32),
        "empty_rows": (2 * B * T + np.arange(SLOTS * P, dtype=np.int32))[:, None],
    }
    nc = bacc.Bacc("TRN2", target_bir_lowering=False, num_devices=1)
    arrays, aps = {}, []
    for name, a in args.items():
        a = np.ascontiguousarray(a)
        arrays[f"in_{name}"] = a
        aps.append(nc.dram_tensor(f"in_{name}", a.shape, mybir.dt.from_np(a.dtype), kind="ExternalInput").ap())
    out = nc.dram_tensor("out", (B, T, D), fp32, kind="ExternalOutput").ap()
    attention_moe_kernel(nc, *aps, out)
    r = run_bass_kernel_spmd(nc, [arrays], core_ids=[0])
    return r.results[0]["out"]
```
